# Optimizing a Trainium2 kernel written in Bass

```python
import numpy as np
import jax
import jax.numpy as jnp

def _softmax(x, axis=-1):
    return jax.nn.softmax(x, axis=axis)

def _gelu(x):
    return jax.nn.gelu(x, approximate=True)

def _silu(x):
    return jax.nn.silu(x)

def _sigmoid(x):
    return jax.nn.sigmoid(x)

def _layernorm(x, axis=-1, eps=1e-05):
    m = jnp.mean(x, axis=axis, keepdims=True)
    v = jnp.var(x, axis=axis, keepdims=True)
    return (x - m) / jnp.sqrt(v + eps)

def _scatter_add(tgt, idx, src, axis=0):
    return tgt.at[idx].add(src)

def _segment_sum(src, seg, n):
    return jax.ops.segment_sum(src, seg, n)
kernel_name = 'mk_xattn_ffn_d1_seqx_r4_f30a45'

def setup_inputs(seed: int=0):
    np.random.seed(seed)
    _w = jnp.asarray

    def _rec_inputs():
        import jax
        import jax.numpy as jnp
        _rk = jax.random.key(seed)
        x = -0.0005207 + 1.001 * jax.random.normal(jax.random.fold_in(_rk, 1), (8, 512, 256), jnp.float32)
        _lenS = 512 - jax.random.randint(jax.random.fold_in(_rk, 7), (8,), 0, max(1, 512 // 4) + 1, jnp.int32)
        _lenS2 = 512 - jax.random.randint(jax.random.fold_in(_rk, 8), (8,), 0, max(1, 512 // 4) + 1, jnp.int32)
        _ctx_1024P = jax.random.normal(jax.random.fold_in(_rk, 11), (8, 16, 256), jnp.float32)
        _ctx_1024c = jax.random.dirichlet(jax.random.fold_in(_rk, 511), 0.3 * jnp.ones((16,), jnp.float32), (8, 512))
        _ctx_1024t = jnp.einsum('bsk,bkd->bsd', _ctx_1024c, _ctx_1024P)
        _ctx_1024t = _ctx_1024t * jax.lax.rsqrt(jnp.mean(jnp.square(_ctx_1024t)) + 1e-12) * 0.953939
        ctx_1024 = 2.81802e-05 + 1.00001 * (_ctx_1024t + 0.3 * jax.random.normal(jax.random.fold_in(_rk, 611), (8, 512, 256), jnp.float32))
        _validS = jnp.arange(512)[None, :] < _lenS[:, None]
        _validS2 = jnp.arange(512)[None, :] < _lenS2[:, None]
        _causal = jnp.tril(jnp.ones((512, 512), dtype=bool))
        mask_Bx1x1xS2_bf1 = jnp.ones((8, 1, 1, 512), dtype=bool)
        return (x, ctx_1024, mask_Bx1x1xS2_bf1)
    x, ctx_1024, mask_Bx1x1xS2_bf1 = _rec_inputs()

    def _L0_xattn_setup():
        import jax, jax.numpy as jnp
        import numpy as np
        D_MODEL = 256
        N_HEADS = 16
        D_HEAD = D_MODEL // N_HEADS

        def _split_heads(x):
            B, L, D = x.shape
            return x.reshape(B, L, N_HEADS, D_HEAD).transpose(0, 2, 1, 3)
        key = jax.random.key(seed)
        ks = jax.random.split(key, 6)
        B, LQ, LK = (4, 128, 1024)
        scale = 1.0 / np.sqrt(D_MODEL)
        return {'q_in': jax.random.normal(ks[0], (B, LQ, D_MODEL), dtype=jnp.float32), 'mem': jax.random.normal(ks[1], (B, LK, D_MODEL), dtype=jnp.float32), 'mem_mask': jnp.ones((B, 1, 1, LK), dtype=bool), 'Wq': jax.random.normal(ks[2], (D_MODEL, D_MODEL), dtype=jnp.float32) * scale, 'Wk': jax.random.normal(ks[3], (D_MODEL, D_MODEL), dtype=jnp.float32) * scale, 'Wv': jax.random.normal(ks[4], (D_MODEL, D_MODEL), dtype=jnp.float32) * scale, 'Wo': jax.random.normal(ks[5], (D_MODEL, D_MODEL), dtype=jnp.float32) * scale}
    _L0_xattn_all = _L0_xattn_setup()
    _L0_xattn_in = {k: v for k, v in _L0_xattn_all.items() if k in ('Wq', 'Wk', 'Wv', 'Wo')}
    del _L0_xattn_all

    def _L0_ffn_setup():
        import jax, jax.numpy as jnp
        import numpy as np
        B, S, D, F, E, K = (2, 512, 256, 1024, 8, 2)
        key = jax.random.key(seed)
        ks = jax.random.split(key, 5)
        x = jax.random.normal(ks[0], (B, S, D), dtype=jnp.float32)
        Wg = jax.random.normal(ks[1], (D, E), dtype=jnp.float32) * 0.02
        W1 = jax.random.normal(ks[2], (E, D, F), dtype=jnp.float32) * 0.02
        b1 = jnp.zeros((E, F), dtype=jnp.float32)
        W2 = jax.random.normal(ks[3], (E, F, D), dtype=jnp.float32) * 0.02
        b2 = jnp.zeros((E, D), dtype=jnp.float32)
        return {'x': x, 'Wg': Wg, 'W1': W1, 'b1': b1, 'W2': W2, 'b2': b2}
    _L0_ffn_all = _L0_ffn_setup()
    _L0_ffn_in = {k: v for k, v in _L0_ffn_all.items() if k in ('Wg', 'W1', 'b1', 'W2', 'b2')}
    del _L0_ffn_all
    return {'x': x, 'ctx_1024': ctx_1024, 'mask_Bx1x1xS2_bf1': mask_Bx1x1xS2_bf1, 'L0_xattn_Wq': _L0_xattn_in['Wq'], 'L0_xattn_Wk': _L0_xattn_in['Wk'], 'L0_xattn_Wv': _L0_xattn_in['Wv'], 'L0_xattn_Wo': _L0_xattn_in['Wo'], 'L0_ffn_Wg': _L0_ffn_in['Wg'], 'L0_ffn_W1': _L0_ffn_in['W1'], 'L0_ffn_b1': _L0_ffn_in['b1'], 'L0_ffn_W2': _L0_ffn_in['W2'], 'L0_ffn_b2': _L0_ffn_in['b2']}

def reference(x, ctx_1024, mask_Bx1x1xS2_bf1, L0_xattn_Wq, L0_xattn_Wk, L0_xattn_Wv, L0_xattn_Wo, L0_ffn_Wg, L0_ffn_W1, L0_ffn_b1, L0_ffn_W2, L0_ffn_b2):
    import jax
    import jax.numpy as jnp

    def _L0_xattn_ref(q_in, mem, mem_mask, Wq, Wk, Wv, Wo):
        import jax, jax.numpy as jnp
        import numpy as np
        D_MODEL = 256
        N_HEADS = 16
        D_HEAD = D_MODEL // N_HEADS

        def _split_heads(x):
            B, L, D = x.shape
            return x.reshape(B, L, N_HEADS, D_HEAD).transpose(0, 2, 1, 3)
        q = _split_heads(q_in @ Wq.T)
        k = _split_heads(mem @ Wk.T)
        v = _split_heads(mem @ Wv.T)
        scores = jnp.einsum('bhqd,bhkd->bhqk', q, k) / jnp.sqrt(jnp.float32(D_HEAD))
        scores = jnp.where(mem_mask, scores, -jnp.inf)
        attn = jax.nn.softmax(scores, axis=-1)
        out = jnp.einsum('bhqk,bhkd->bhqd', attn, v)
        B, H, LQ, Dh = out.shape
        out = out.transpose(0, 2, 1, 3).reshape(B, LQ, H * Dh)
        return out @ Wo.T

    def _L0_ffn_ref(x, Wg, W1, b1, W2, b2):
        import jax, jax.numpy as jnp
        import numpy as np
        B, S, D, F, E, K = (2, 512, 256, 1024, 8, 2)
        b, s, d = x.shape
        e = Wg.shape[1]
        T = b * s
        C = 2 * K * T // e
        xt = x.reshape(T, d)
        logits = xt.astype(jnp.float32) @ Wg.astype(jnp.float32)
        gates = jax.nn.softmax(logits, axis=-1)
        idx1 = jnp.argmax(gates, axis=-1)
        mask1 = jax.nn.one_hot(idx1, e, dtype=gates.dtype)
        gate1 = jnp.sum(gates * mask1, axis=-1)
        logits2 = jnp.where(mask1 > 0, -jnp.inf, logits)
        idx2 = jnp.argmax(logits2, axis=-1)
        mask2 = jax.nn.one_hot(idx2, e, dtype=gates.dtype)
        gate2 = jnp.sum(gates * mask2, axis=-1)
        denom = gate1 + gate2 + 1e-09
        w1 = gate1 / denom
        w2 = gate2 / denom
        p1 = jnp.cumsum(mask1, axis=0) - mask1
        pos1 = jnp.sum(p1 * mask1, axis=-1).astype(jnp.int32)
        off = jnp.sum(mask1, axis=0)
        p2 = jnp.cumsum(mask2, axis=0) - mask2 + off[None, :]
        pos2 = jnp.sum(p2 * mask2, axis=-1).astype(jnp.int32)
        keep1 = (pos1 < C).astype(xt.dtype)
        keep2 = (pos2 < C).astype(xt.dtype)
        pos1 = jnp.clip(pos1, 0, C - 1)
        pos2 = jnp.clip(pos2, 0, C - 1)
        xe = jnp.zeros((e, C, d), dtype=xt.dtype)
        xe = xe.at[idx1, pos1].add(xt * keep1[:, None])
        xe = xe.at[idx2, pos2].add(xt * keep2[:, None])
        h = jax.nn.gelu(jnp.einsum('ecd,edf->ecf', xe, W1) + b1[:, None, :], approximate=False)
        ye = jnp.einsum('ecf,efd->ecd', h, W2) + b2[:, None, :]
        out = ye[idx1, pos1] * (w1 * keep1)[:, None] + ye[idx2, pos2] * (w2 * keep2)[:, None]
        return out.reshape(b, s, d)
    x = x + _L0_xattn_ref(_layernorm(x, axis=-1), ctx_1024, mask_Bx1x1xS2_bf1, L0_xattn_Wq, L0_xattn_Wk, L0_xattn_Wv, L0_xattn_Wo)
    x = x + _L0_ffn_ref(_layernorm(x, axis=-1), L0_ffn_Wg, L0_ffn_W1, L0_ffn_b1, L0_ffn_W2, L0_ffn_b2)
    return x

_drawn_inputs = setup_inputs


def setup_inputs(seed=0):
    import zlib

    import numpy as np

    out = dict(_drawn_inputs(seed))
    spreads = {'L0_ffn_b1': (0.0, 0.346), 'L0_ffn_b2': (0.0, 0.1)}
    factors = {}
    for name, (base, spread) in spreads.items():
        noise = np.random.default_rng([zlib.crc32(name.encode()), seed]).standard_normal(out[name].shape)
        drawn = base * np.exp(spread * noise) if base else spread * noise
        out[name] = jnp.asarray(drawn.astype(out[name].dtype))
    for name, factor in factors.items():
        out[name] = (out[name] * factor).astype(out[name].dtype)
    return out
```

```python
from contextlib import ExitStack

import concourse.bass as bass
from concourse import mybir

F32 = mybir.dt.float32
F32R = mybir.dt.float32r
I32 = mybir.dt.int32
U32 = mybir.dt.uint32
U8 = mybir.dt.uint8
ALU = mybir.AluOpType
ACT = mybir.ActivationFunctionType
AX = mybir.AxisListType.X

P = 128
NB, T, D = 8, 512, 256
NH, DH = 16, 16
G = 4
NG = NH // G
QT = T // P
KD = D // P
E, FF = 8, 1024
KF = FF // P
CAP = 2 * 2 * NB * T // E
REGION = NB * T
NREG = 2 * E
NTOK = NB * T
TILES = (2 * NTOK - E) // P + E
LEAD = 6
STEPS = NG * QT
SCALE = DH ** -0.5
EPS = 1e-5
BIG = 3e38
RING = 4
SROWS, TROWS = 96, 98

JOBS = {0: ["T0n", "T1n"], 1: ["V1"], 2: ["R1"], 3: ["Q0n"], 4: ["K0n"], 5: ["K1n"], 6: ["R2"], 7: ["Q1n"],
        8: ["O0p"], 9: ["O1p"], 10: ["R3"], 11: ["V0n"], 12: ["U0p", "U1p"], 13: ["Lp"], 14: ["R0n"],
        15: ["Pp"]}
AHEAD = ["T0n", "T1n", "Q0n", "K0n", "K1n", "Q1n", "V0n", "R0n"]
NORM_STEPS = [4, 5, 6, 10]
FIRST, MID, LAST, TAIL = range(4)


def jobs_of(kind):
    if kind == TAIL:
        return ["O0p", "O1p", "U0p", "U1p", "Lp", "Pp"]
    return [n for j in sorted(JOBS) for n in JOBS[j]
            if not (kind == FIRST and n[-1] == "p") and not (kind == LAST and n[-1] == "n")]


PER = len(jobs_of(MID))


def number(b, kind, name):
    before = len(AHEAD) + (0 if kind == FIRST else len(jobs_of(FIRST)) - PER)
    if kind == TAIL:
        return before + (NB - 1) * PER + len(jobs_of(LAST)) + jobs_of(kind).index(name)
    return before + b * PER + jobs_of(kind).index(name)


def build(nc, x, ctxT, mask, WqT, WkT, WvT, WoT, Wg, W1, b1, W2, b2, out):
    with ExitStack() as ctx:
        def sem(name):
            return ctx.enter_context(nc.semaphore(name))

        place = [nc.sbuf_base + (-nc.sbuf_base) % 64]
        ctx.enter_context(nc.sbuf_tensor("arena", [P, (nc.sbuf_usable_end - place[0]) // 4 - 16], F32))

        def at(name, shape, dt=F32):
            n = 1 if dt == U8 else 4
            for s in shape[1:]:
                n *= s
            t = nc.alloc_sbuf_tensor_at(name, shape, dt, offset=place[0])
            place[0] += n + (-n) % 32
            return t

        b1r = at("b1r", [P, E, FF])
        b2r = at("b2r", [P, E, D])
        ident = at("ident", [P, P])
        upper = at("upper", [P, P])
        ones = at("ones", [P, P])
        rev = at("rev", [P, QT, E])
        count = at("count", [P, 2, E])
        wg_sb = at("wg_sb", [P, KD, E])
        mhalf = at("mhalf", [P, QT])
        expert_i = at("expert_i", [P, TILES], I32)
        rows_i = at("rows_i", [P, TILES + RING], I32)
        pick = at("pick", [P, TILES, 2])
        base = at("base", [P, 2, E])
        tio = at("tio", [P, TILES])
        pio = at("pio", [P, 1])
        eio = at("eio", [P, E])
        ex = at("ex", [P, 10, E])
        nint = at("nint", [P, E], I32)
        shared = place[0]
        X = at("X", [P, RING, D])
        meta_in = at("meta_in", [P, RING, 4])
        rowidx = at("rowidx", [P, RING], I32)
        XT = at("XT", [P, KD, P])
        hb = at("hb", [P, FF])
        hg = at("hg", [P, FF])
        hT = at("hT", [P, KF, P])
        y = at("y", [P, 2, D])
        y0 = at("y0", [P, D])
        wpair = at("wpair", [P, 2, 2])
        wcol = at("wcol", [P, 2])
        ffn_end = place[0]
        place[0] = shared
        wo_sb = at("wo_sb", [P, KD, D])
        big = nc.alloc_sbuf_tensor_at("big", [P, 2, TILES, E], F32, offset=place[0])
        tab = nc.alloc_sbuf_tensor_at("tab", [P, 10, TILES], F32, offset=place[0] + 4 * 2 * TILES * E)
        oN = at("oN", [P, 2, T])
        oT = at("oT", [P, 2, T])
        rb = at("rb", [P, 2, T])
        mask_f = nc.alloc_sbuf_tensor_at("mask_f", [NB, T], F32, offset=place[0])
        mask_u8 = nc.alloc_sbuf_tensor_at("mask_u8", [NB, T], U8, offset=place[0] + 4 * T)
        xR = at("xR", [P, QT, D])
        x1 = at("x1", [P, QT, D])
        h2 = at("h2", [P, QT, D])
        h2T = at("h2T", [P, KD, T])
        den = at("den", [P, NH * T // P])
        rden = at("rden", [P, NH * T // P])
        meta = at("meta", [P, QT, 4])
        ridx = at("ridx", [P, 2, QT], I32)
        small = at("small", [P, 16, QT * E])
        choice = at("choice", [P, 2, QT, E])
        col = at("col", [P, 12, QT])
        idf = at("idf", [P, QT])
        bst = at("bst", [P, QT, 6])
        mv2 = at("mv2", [P, QT, 2])
        r2 = at("r2", [P, QT])
        prefix = at("prefix", [P, 2, 2, QT, E])
        basis = at("basis", [P, 2, QT, E])
        place[0] = max(place[0], ffn_end)
        upto = place[0]
        W1s = at("W1s", [P, E, KD, FF])
        W2s = at("W2s", [P, E, KF, D])
        weights_end = place[0]
        place[0] = upto
        Qs = at("Qs", [TROWS, NG, G, T])
        Ks = at("Ks", [TROWS, NG, G, T])
        probs = at("probs", [P, 2, G, T])
        V = at("V", [P, QT, NH, 2 * DH])
        wq_sb = at("wq_sb", [P, KD, D])
        wk_sb = at("wk_sb", [P, KD, D])
        wv_sb = at("wv_sb", [P, KD, D])
        xA = at("xA", [P, QT, D])
        xnT = at("xnT", [P, KD, T])
        cT = at("cT", [P, KD, T])
        Qhi = at("Qhi", [P, 2, T])
        Qlo = at("Qlo", [P, 2, T])
        Khi = at("Khi", [P, 2, T])
        Klo = at("Klo", [P, 2, T])
        oraw = at("oraw", [P, 2, T])
        negmax = at("negmax", [P, 2, G * QT])
        mhi = at("mhi", [G * QT, 2, P])
        mlo = at("mlo", [G * QT, 2, P])
        ast = at("ast", [P, QT, 6])
        mv1 = at("mv1", [P, QT, 2])
        r1 = at("r1", [P, QT])
        attention_end = place[0]
        fill0 = nc.alloc_sbuf_tensor_at("fill0", [P, NREG * REGION // P, 4], F32, offset=upto)
        assert max(weights_end, attention_end) <= nc.sbuf_usable_end - 64

        psMax = ctx.enter_context(nc.psum_tensor("psMax", [P, 2, 512], F32))
        psT = ctx.enter_context(nc.psum_tensor("psT", [P, 4, 512], F32))
        psO = ctx.enter_context(nc.psum_tensor("psO", [P, 512], F32))
        psM = ctx.enter_context(nc.psum_tensor("psM", [P, 512], F32))

        qd = nc.dram_tensor("qd", [3 * DH, NH, T], F32, kind="Internal").ap()
        kd = nc.dram_tensor("kd", [NB, 2 * DH + 1, NH, T], F32, kind="Internal").ap()
        od = nc.dram_tensor("od", [NH, 2 * DH, T], F32, kind="Internal").ap()
        rdend = nc.dram_tensor("rdend", [NH, T], F32, kind="Internal").ap()
        table = nc.dram_tensor("table", [NREG * REGION + P, 4], F32, kind="Internal").ap()
        h2d = nc.dram_tensor("h2d", [NTOK + P, D], F32, kind="Internal").ap()

        pool_step = sem("pool_step")
        sp_step = sem("sp_step")
        wload = sem("wload")
        bload = sem("bload")
        setup = sem("setup")
        vset = sem("vset")
        maskst = sem("maskst")
        xa_in = sem("xa_in")
        ct_in = sem("ct_in")
        xr_in = sem("xr_in")
        ln1_stat = sem("ln1_stat")
        ln1_rs = sem("ln1_rs")
        ln1 = sem("ln1")
        job_mm = sem("job_mm")
        job_rd = sem("job_rd")
        hi_done = sem("hi_done")
        filled = [sem(f"filled{g}") for g in range(NG)]
        mrow = [sem(f"mrow{g}") for g in range(NG)]
        smax_mm = sem("smax_mm")
        max_rd = sem("max_rd")
        st_mm = sem("st_mm")
        exp_rd = sem("exp_rd")
        pv_mm = sem("pv_mm")
        o_copy = sem("o_copy")
        o_out = [sem(f"o_out{i}") for i in range(2)]
        ot_in = sem("ot_in")
        stored = [sem(f"stored{i}") for i in range(2)]
        den_in = sem("den_in")
        den_rd = sem("den_rd")
        den_st = sem("den_st")
        rb_in = sem("rb_in")
        o_norm = sem("o_norm")
        x1_done = sem("x1_done")
        ln2_stat = sem("ln2_stat")
        ln2_rs = sem("ln2_rs")
        ln2 = sem("ln2")
        x1_st = sem("x1_st")
        shifted = sem("shifted")
        gate_exp = sem("gate_exp")
        choice_done = sem("choice_done")
        route = sem("route")
        empty_st = sem("empty_st")
        scat = sem("scat")
        tiles_done = sem("tiles_done")
        w_in = sem("w_in")
        tio_done = sem("tio_done")
        rix = sem("rix")
        g_meta = [sem(f"g_meta{i}") for i in range(RING)]
        g_x = [sem(f"g_x{i}") for i in range(RING)]
        x_tr = sem("x_tr")
        x_trc = sem("x_trc")
        h_mm = sem("h_mm")
        h_b = sem("h_b")
        h_g = sem("h_g")
        h_tr = sem("h_tr")
        h_trc = sem("h_trc")
        h_trd = sem("h_trd")
        y_mm = sem("y_mm")
        y_done = sem("y_done")
        added = sem("added")

        def wait(eng, s, value):
            if not isinstance(value, int) or value > 0:
                eng.wait_ge(s, value)

        def batches(eng, body):
            body(0, FIRST)
            body(1, MID)
            with eng.Fori(2, NB - 1) as b:
                body(b, MID)
            body(NB - 1, LAST)

        def tiles(eng, body):
            rounds = (TILES - 4) // RING
            body(0, 0, 0)
            body(1, 1, 0)
            with eng.Fori(0, rounds) as i:
                for u in range(2, RING + 2):
                    body(i * RING + u, u % RING, i + u // RING)
            for t in range(rounds * RING + 2, TILES):
                body(t, t % RING, t // RING)

        FILLS = 16 * 4
        STORES = 16 * 5
        ROWS4 = (lambda b: x[b].rearrange("(t p) d -> p t d", p=P))

        block = ctx.enter_context(nc.Block())

        @block.sync
        def _(sp):
            def store_parts(b, half):
                hs = slice(half * 8, half * 8 + 8)

                def put(dst, r, part):
                    sp.dma_start(dst[r:r + DH, hs, :].rearrange("d h n -> h d n"),
                                 part[:, half, :]).then_inc(stored[half], 16)
                put(qd, 0, Qhi)
                put(qd, DH, Qlo)
                put(qd, 2 * DH, Qhi)
                put(kd[b], 0, Khi)
                put(kd[b], DH, Klo)

            def fill(b, g):
                sp.sem_inc(sp_step, 1)
                sp.wait_ge(stored[g // 2], STORES * (b + 1))
                hs = slice(g * G, g * G + G)
                for r, src in ((0, qd[0:32, hs, :]), (32, qd[16:48, hs, :])):
                    sp.dma_start(Qs[r:r + 32, g, :, :], src).then_inc(filled[g], 16)
                for r, n in ((0, 32), (32, 33)):
                    sp.dma_start(Ks[r:r + n, g, :, :], kd[b][0:n, hs, :]).then_inc(filled[g], 16)

            def store_out(g):
                sp.dma_start(od[g * G:g * G + G, :, :].rearrange("h r n -> (h r) n"),
                             oraw[:, g % 2, :]).then_inc(o_out[g % 2], 16)

            def put_max(g):
                i = g % 2
                sp.dma_start(Qs[96:97, g, :, :], mhi[:, i, :]).then_inc(mrow[g], 16)
                sp.dma_start(Qs[97:98, g, :, :], mlo[:, i, :]).then_inc(mrow[g], 16)

            def out_load(n):
                sp.wait_ge(o_out[0], 32 * n)
                sp.wait_ge(o_out[1], 32 * n)
                sp.dma_start(den[:, :], od[:, DH, :].rearrange("h (a n) -> h a n", n=NH * T // P)).then_inc(den_in, 16)
                wait(sp, o_norm, 2 * (n - 1))
                for half in range(2):
                    sp.dma_start(oT[:, half, :], od[half * 8:half * 8 + 8, 0:DH, :]).then_inc(ot_in, 16)

            def den_back(n):
                sp.wait_ge(den_rd, n)
                sp.dma_start(rdend.rearrange("h (a n) -> h a n", n=NH * T // P), rden[:, :]).then_inc(den_st, 16)
                sp.wait_ge(den_st, 16 * n)
                for half in range(2):
                    sp.dma_start(rb[:, half, :], rdend[half * 8:half * 8 + 8].unsqueeze(1).to_broadcast(
                        [8, DH, T])).then_inc(rb_in, 16)

            sp.dma_start(xA[:, :, :], ROWS4(0)).then_inc(xa_in, 16)
            sp.dma_start(mask_u8[:, :], mask).then_inc(wload, 16)
            for dst, src in ((wq_sb, WqT), (wk_sb, WkT), (wv_sb, WvT), (wo_sb, WoT), (wg_sb, Wg)):
                sp.dma_start(dst[:, :, :], src.rearrange("(k p) n -> p k n", p=P)).then_inc(wload, 16)
            sp.dma_start(cT[:, :, :], ctxT[0].rearrange("(k p) n -> p k n", p=P)).then_inc(ct_in, 16)
            sp.wait_ge(vset, 1)
            sp.dma_start(kd[:, 2 * DH, :, :], mask_f[:, :].unsqueeze(1).to_broadcast([NB, NH, T])).then_inc(maskst, 16)
            sp.wait_ge(vset, 2)
            sp.wait_ge(job_rd, 2)
            sp.dma_start(xA[:, :, :], ROWS4(1)).then_inc(xa_in, 16)
            sp.wait_ge(job_rd, 6)
            store_parts(0, 0)
            store_parts(0, 1)
            sp.wait_ge(maskst, 16)
            for g in range(NG):
                fill(0, g)
            sp.wait_ge(job_rd, 8)
            put_max(0)

            def body(b, kind):
                num = lambda name: number(b, kind, name)
                if kind != LAST:
                    sp.wait_ge(job_rd, num("T1n") + 1)
                    sp.dma_start(xA[:, :, :], ROWS4((b + 2) % NB)).then_inc(xa_in, 16)
                if kind != FIRST:
                    sp.wait_ge(st_mm, 32 * b)
                    fill(b, 3)
                    sp.wait_ge(o_copy, 4 * b)
                    store_out(3)
                if kind != LAST:
                    sp.wait_ge(job_rd, num("V1") + 1)
                    sp.dma_start(cT[:, :, :], ctxT[b + 1].rearrange("(k p) n -> p k n", p=P)).then_inc(ct_in, 16)
                if kind != FIRST:
                    out_load(b)
                sp.wait_ge(job_rd, num("R1") + 1)
                put_max(1)
                if kind != FIRST:
                    wait(sp, x1_done, 2 * (b - 1))
                    sp.dma_start(xR[:, :, :], ROWS4(b - 1)).then_inc(xr_in, 16)
                    den_back(b)
                    sp.wait_ge(ot_in, 32 * b)
                    sp.sem_inc(sp_step, 1)
                sp.wait_ge(o_copy, 4 * b + 1)
                store_out(0)
                if kind != LAST:
                    sp.wait_ge(job_rd, num("K0n") + 1)
                    sp.sem_inc(sp_step, 1)
                    sp.wait_ge(filled[1], FILLS * (b + 1))
                    store_parts(b + 1, 0)
                sp.wait_ge(job_rd, num("R2") + 1)
                put_max(2)
                if kind != LAST:
                    sp.wait_ge(st_mm, 32 * b + 8)
                    fill(b + 1, 0)
                    sp.wait_ge(job_rd, num("Q1n") + 1)
                    sp.wait_ge(filled[3], FILLS * (b + 1))
                    store_parts(b + 1, 1)
                    sp.wait_ge(st_mm, 32 * b + 16)
                    fill(b + 1, 1)
                sp.wait_ge(o_copy, 4 * b + 2)
                store_out(1)
                sp.wait_ge(job_rd, num("R3") + 1)
                put_max(3)
                if kind != LAST:
                    sp.wait_ge(st_mm, 32 * b + 24)
                    fill(b + 1, 2)
                sp.wait_ge(o_copy, 4 * b + 3)
                store_out(2)
                if kind != LAST:
                    sp.wait_ge(job_rd, num("R0n") + 1)
                    put_max(0)

            batches(sp, body)
            sp.wait_ge(o_copy, 4 * NB)
            store_out(3)
            out_load(NB)
            sp.wait_ge(x1_done, 2 * (NB - 1))
            sp.dma_start(xR[:, :, :], ROWS4(NB - 1)).then_inc(xr_in, 16)
            den_back(NB)
            sp.wait_ge(pv_mm, 16 * NB)
            for e in range(E):
                sp.dma_start(W1s[:, e, :, :], W1[e].rearrange("(k p) f -> p k f", p=P)).then_inc(w_in, 16)
                sp.dma_start(W2s[:, e, :, :], W2[e].rearrange("(k p) n -> p k n", p=P)).then_inc(w_in, 16)

        @block.tensor
        def _(pe):
            def scores_max(b, h, qt):
                g, hh = h // G, h % G
                if qt == 0 and hh == 0:
                    pe.wait_ge(filled[g], FILLS * (b + 1))
                wait(pe, max_rd, 4 * (NH * b + h) + qt - 1)
                nc.tensor.matmul(psMax[:, qt % 2, :], Qs[0:SROWS, g, hh, qt * P:(qt + 1) * P].bitcast(F32R),
                                 Ks[0:SROWS, g, hh, :].bitcast(F32R), start=True, stop=True).then_inc(smax_mm, 1)

            def scores_t(b, j, pair):
                g, kt = j // QT, j % QT
                if kt == 0 and pair == 0:
                    pe.wait_ge(mrow[g], 32 * (b + 1))
                wait(pe, exp_rd, 32 * b + 2 * j + pair - 1)
                for hh in (2 * pair, 2 * pair + 1):
                    last = nc.tensor.matmul(psT[:, hh, :], Ks[0:TROWS, g, hh, kt * P:(kt + 1) * P].bitcast(F32R),
                                            Qs[0:TROWS, g, hh, :].bitcast(F32R), start=True, stop=True)
                last.then_inc(st_mm, 1)

            def values(b, j):
                g, kt = j // QT, j % QT
                pe.wait_ge(exp_rd, 2 * (STEPS * b + j) + 2)
                if kt == 0:
                    wait(pe, o_copy, NG * b + g)
                for hh in range(G):
                    last = nc.tensor.matmul(psO[32 * hh:32 * hh + 32, :], V[:, kt, g * G + hh, :],
                                            probs[:, j % 2, hh, :], start=(kt == 0), stop=(kt == QT - 1))
                last.then_inc(pv_mm, 1)

            def job(b, kind, name, n=None):
                n = number(b, kind, name) if n is None else n
                wait(pe, job_rd, n)
                what = name[0]
                if what == "T":
                    k = int(name[1])
                    if k == 0:
                        pe.wait_ge(ln1, b + 2)
                    for i in range(QT):
                        last = nc.tensor.transpose(psM[:, i * P:(i + 1) * P], xA[:, i, k * P:(k + 1) * P], ident[:, :])
                elif what in "QK":
                    half = int(name[1])
                    w, src = (wq_sb, xnT) if what == "Q" else (wk_sb, cT)
                    if name[:2] == "K0":
                        pe.wait_ge(ct_in, 16 * (b + 2))
                    for k in range(KD):
                        last = nc.tensor.matmul(psM[:, :], w[:, k, half * P:(half + 1) * P], src[:, k, :],
                                                start=(k == 0), stop=(k == KD - 1))
                elif what == "V":
                    half = int(name[1])
                    for kt in range(QT):
                        for k in range(KD):
                            last = nc.tensor.matmul(psM[:, kt * P:(kt + 1) * P], cT[:, k, kt * P:(kt + 1) * P],
                                                    wv_sb[:, k, half * P:(half + 1) * P],
                                                    start=(k == 0), stop=(k == KD - 1))
                elif what == "R":
                    g = int(name[1])
                    nb = b + 1 if name[-1] == "n" else b
                    pe.wait_ge(max_rd, 4 * (NH * nb + G * g + G))
                    last = nc.tensor.transpose(psM[0:G * QT, 0:P], negmax[:, g % 2, :], ident[:, :])
                elif what == "O":
                    i = int(name[1])
                    if i == 0:
                        pe.wait_ge(o_norm, 2 * b)
                    for c in range(2):
                        qt = 2 * i + c
                        for k in range(KD):
                            last = nc.tensor.matmul(psM[:, c * D:(c + 1) * D], oN[:, k, qt * P:(qt + 1) * P],
                                                    wo_sb[:, k, :], start=(k == 0), stop=(k == KD - 1))
                elif what == "U":
                    k = int(name[1])
                    if k == 0:
                        pe.wait_ge(ln2, b)
                    for i in range(QT):
                        last = nc.tensor.transpose(psM[:, i * P:(i + 1) * P], h2[:, i, k * P:(k + 1) * P], ident[:, :])
                elif what == "L":
                    for qt in range(QT):
                        for k in range(KD):
                            last = nc.tensor.matmul(psM[:, qt * E:(qt + 1) * E], h2T[:, k, qt * P:(qt + 1) * P],
                                                    wg_sb[:, k, :], start=(k == 0), stop=(k == KD - 1))
                else:
                    pe.wait_ge(choice_done, b)
                    n = 2 * QT * E
                    nc.tensor.matmul(psM[:, 0:n], upper[:, :], choice[:, :, :, :], start=True, stop=True)
                    last = nc.tensor.matmul(psM[:, n:2 * n], ones[:, :], choice[:, :, :, :], start=True, stop=True)
                last.then_inc(job_mm, 1)

            pe.wait_ge(setup, 1)
            pe.wait_ge(wload, 16 * 6)
            pe.wait_ge(ct_in, 16)
            for n, name in enumerate(AHEAD[:-1]):
                job(-1, FIRST, name, n)
            for h in range(LEAD):
                for qt in range(QT):
                    scores_max(0, h, qt)
                if h == G - 1:
                    job(-1, FIRST, "R0n", len(AHEAD) - 1)

            def body(b, kind):
                names = jobs_of(kind)
                for j in range(STEPS):
                    h = j + LEAD
                    ahead = h < NH or kind != LAST
                    hb_ = b + h // NH
                    if ahead:
                        scores_max(hb_, h % NH, 0)
                    scores_t(b, j, 0)
                    if ahead:
                        scores_max(hb_, h % NH, 1)
                    scores_t(b, j, 1)
                    if ahead:
                        scores_max(hb_, h % NH, 2)
                    for name in JOBS.get(j, []):
                        if name in names:
                            job(b, kind, name)
                    if ahead:
                        scores_max(hb_, h % NH, 3)
                    if j > 0:
                        values(b, j - 1)
                    elif kind != FIRST:
                        values(b - 1, STEPS - 1)
            batches(pe, body)
            values(NB - 1, STEPS - 1)
            for name in jobs_of(TAIL):
                job(NB, TAIL, name)

            def expert_of(t):
                return pe.value_load(expert_i[0:1, bass.ds(t, 1)], min_val=0, max_val=E - 1)

            def transpose_tokens(t, u, r):
                pe.wait_ge(g_x[u], 16 * (r + 1))
                wait(pe, x_trc, t)
                for k in range(KD):
                    last = nc.tensor.transpose(psM[:, k * P:(k + 1) * P], X[:, u, k * P:(k + 1) * P], ident[:, :])
                last.then_inc(x_tr, 1)

            def first_product(t, half, e):
                pe.wait_ge(x_trc, t + 1)
                wait(pe, h_b, 2 * t - 1 + half)
                for k in range(KD):
                    last = nc.tensor.matmul(psT[:, half, :], XT[:, k, :],
                                            W1s[:, bass.ds(e, 1), k, half * 512:(half + 1) * 512],
                                            start=(k == 0), stop=(k == KD - 1))
                last.then_inc(h_mm, 1)

            def transpose_hidden(t):
                for half, copied in enumerate((h_trc, h_trd)):
                    pe.wait_ge(h_g, 2 * t + half + 1)
                    wait(pe, copied, t)
                    for k in range(4):
                        c = 4 * half + k
                        last = nc.tensor.transpose(psT[:, 2 + half, k * P:(k + 1) * P], hg[:, c * P:(c + 1) * P],
                                                   ident[:, :])
                    last.then_inc(h_tr, 1)

            def second_product(t, u, e):
                wait(pe, y_done, t - 1)
                for half, copied in enumerate((h_trc, h_trd)):
                    pe.wait_ge(copied, t + 1)
                    for k in range(4):
                        c = 4 * half + k
                        last = nc.tensor.matmul(psMax[:, u % 2, 0:D], hT[:, c, :], W2s[:, bass.ds(e, 1), c, :],
                                                start=(c == 0), stop=(c == KF - 1))
                last.then_inc(y_mm, 1)

            pe.wait_ge(tiles_done, 1)
            transpose_tokens(0, 0, 0)
            pe.wait_ge(w_in, 16 * 2 * E)
            e0 = expert_of(0)
            first_product(0, 0, e0)
            first_product(0, 1, e0)
            transpose_tokens(1, 1, 0)

            def expert_step(t, u, r):
                more = not isinstance(t, int) or t + 1 < TILES
                if more:
                    e1 = expert_of(t + 1)
                    first_product(t + 1, 0, e1)
                transpose_hidden(t)
                if more:
                    first_product(t + 1, 1, e1)
                if not isinstance(t, int) or t + 2 < TILES:
                    transpose_tokens(t + 2, (u + 2) % RING, r + (u + 2) // RING)
                second_product(t, u, expert_of(t))

            tiles(pe, expert_step)

        @block.scalar
        def _(act):
            def exp_step(b, j):
                n = STEPS * b + j
                for pair in range(2):
                    act.wait_ge(st_mm, 2 * n + pair + 1)
                    if pair == 0:
                        wait(act, pv_mm, n - 1)
                    nc.scalar.activation(probs[:, j % 2, 2 * pair:2 * pair + 2, :], psT[:, 2 * pair:2 * pair + 2, :],
                                         ACT.Exp, scale=SCALE).then_inc(exp_rd, 1)

            def out_copy(b, g):
                n = NG * b + g
                act.wait_ge(pv_mm, QT * n + QT)
                if not isinstance(b, int) or n >= 2:
                    k = b * 2 + g // 2
                    act.wait_ge(o_out[g % 2], 16 * k)
                nc.scalar.copy(oraw[:, g % 2, :], psO[:, :]).then_inc(o_copy, 1)

            def job(b, kind, name, n=None):
                n = number(b, kind, name) if n is None else n
                what = name[0]
                if what not in "TQKVU":
                    return
                act.wait_ge(job_mm, n + 1)
                i = int(name[1])
                if what == "T":
                    nc.scalar.copy(xnT[:, i, :], psM[:, :]).then_inc(job_rd, 1)
                elif what == "U":
                    nc.scalar.copy(h2T[:, i, :], psM[:, :]).then_inc(job_rd, 1)
                elif what == "V":
                    nc.scalar.copy(V[:, :, i * 8:(i + 1) * 8, 0:DH],
                                   psM[:, :].rearrange("p (t h d) -> p t h d", t=QT, d=DH)).then_inc(job_rd, 1)
                else:
                    wait(act, stored[i], STORES * (b + 1))
                    dst = Qhi if what == "Q" else Khi
                    nc.scalar.copy(dst[:, i, :].bitcast(F32R), psM[:, :]).then_inc(hi_done, 1)

            act.dma_start(b1r[:, :, :].rearrange("p e f -> p (e f)"), b1.partition_broadcast(P)).then_inc(bload, 16)
            act.dma_start(b2r[:, :, :].rearrange("p e f -> p (e f)"), b2.partition_broadcast(P)).then_inc(bload, 16)
            act.wait_ge(vset, 2)
            for n, name in enumerate(AHEAD[:-1]):
                job(-1, FIRST, name, n)

            def body(b, kind):
                names = jobs_of(kind)
                for j in range(STEPS):
                    exp_step(b, j)
                    for name in JOBS.get(j, []):
                        if name in names:
                            job(b, kind, name)
                            if name == "Lp":
                                gate(b)
                    if j % QT == 0:
                        if j > 0:
                            out_copy(b, j // QT - 1)
                        elif kind != FIRST:
                            out_copy(b - 1, NG - 1)

            def gate(n):
                act.wait_ge(shifted, n)
                nc.scalar.activation(small[:, 2, :], small[:, 1, :], ACT.Exp).then_inc(gate_exp, 1)

            batches(act, body)
            out_copy(NB - 1, NG - 1)
            for name in jobs_of(TAIL):
                job(NB, TAIL, name)
                if name == "Lp":
                    gate(NB)

            def tokens_copy(t):
                act.wait_ge(x_tr, t + 1)
                wait(act, h_mm, 2 * t)
                nc.scalar.copy(XT[:, :, :], psM[:, 0:D].rearrange("p (k n) -> p k n", k=KD)).then_inc(x_trc, 1)

            def expert_step(t, u, r):
                for half in range(2):
                    act.wait_ge(h_b, 2 * t + half + 1)
                    wait(act, h_tr, 2 * t - 1 + half)
                    nc.scalar.activation(hg[:, half * 512:(half + 1) * 512], hb[:, half * 512:(half + 1) * 512],
                                         ACT.Gelu).then_inc(h_g, 1)
                act.wait_ge(h_tr, 2 * t + 1)
                wait(act, y_mm, t)
                nc.scalar.copy(hT[:, 0:4, :], psT[:, 2, :].rearrange("p (k n) -> p k n", k=4)).then_inc(h_trc, 1)
                if not isinstance(t, int) or t + 2 < TILES:
                    tokens_copy(t + 2)

            tokens_copy(0)
            tokens_copy(1)
            tiles(act, expert_step)

        @block.vector
        def _(dve):
            v = nc.vector

            def statistics(src, st, mv, i):
                v.bn_stats(st[:, i, :], src[:, i, :])
                dve.drain()
                return v.bn_aggr(mv[:, i, :], st[:, i, :])

            def finish_statistics(mv, done):
                dve.drain()
                v.tensor_scalar(mv[:, :, 1:2], mv[:, :, 1:2], EPS, None, ALU.add).then_inc(done, 1)

            def normalise(dst, src, mv, rs, i):
                return v.tensor_scalar(dst[:, i, :], src[:, i, :], mv[:, i, 0:1], rs[:, i:i + 1],
                                       ALU.subtract, ALU.mult)

            def take_max(b, h, qt):
                g, hh = h // G, h % G
                dve.wait_ge(smax_mm, 4 * (NH * b + h) + qt + 1)
                v.tensor_reduce(negmax[:, g % 2, hh * QT + qt:hh * QT + qt + 1], psMax[:, qt % 2, :], AX, ALU.max,
                                negate=True).then_inc(max_rd, 1)

            def job(b, kind, name, n=None):
                n = number(b, kind, name) if n is None else n
                what = name[0]
                if what in "TUV":
                    return
                dve.wait_ge(job_mm, n + 1)
                i = int(name[1]) if what not in "LP" else 0
                if what in "QK":
                    before = 0 if isinstance(b, int) and b < 0 else 4 * (b + 1)
                    mine = {"Q0": 1, "K0": 2, "K1": 3, "Q1": 4}[name[:2]]
                    dve.wait_ge(hi_done, before + mine)
                    hi, lo = (Qhi, Qlo) if what == "Q" else (Khi, Klo)
                    v.tensor_tensor(lo[:, i, :].bitcast(F32R), psM[:, :], hi[:, i, :], ALU.subtract).then_inc(job_rd, 1)
                elif what == "R":
                    nb = b + 1 if name[-1] == "n" else b
                    wait(dve, mrow[(i + 2) % NG], 32 * (nb + i // 2))
                    v.tensor_copy(mhi[:, i % 2, :].bitcast(F32R), psM[0:G * QT, 0:P])
                    dve.drain()
                    v.tensor_tensor(mlo[:, i % 2, :].bitcast(F32R), psM[0:G * QT, 0:P], mhi[:, i % 2, :],
                                    ALU.subtract).then_inc(job_rd, 1)
                elif what == "O":
                    if i == 0:
                        dve.wait_ge(xr_in, 16 * b)
                        wait(dve, x1_st, 32 * (b - 1))
                    v.tensor_tensor(x1[:, 2 * i:2 * i + 2, :], psM[:, :].rearrange("p (t d) -> p t d", t=2),
                                    xR[:, 2 * i:2 * i + 2, :], ALU.add).then_inc(x1_done, 1)
                    dve.wait_ge(x1_done, 2 * (b - 1) + i + 1)
                    statistics(x1, bst, mv2, 2 * i).then_inc(job_rd, 1)
                    statistics(x1, bst, mv2, 2 * i + 1)
                    if i == 1:
                        finish_statistics(mv2, ln2_stat)
                elif what == "L":
                    v.tensor_copy(small[:, 0, :], psM[:, 0:QT * E]).then_inc(job_rd, 1)
                else:
                    v.tensor_copy(prefix[:, :, :, :, :], psM[:, 0:4 * QT * E].rearrange(
                        "p (a k t e) -> p a k t e", a=2, k=2, t=QT)).then_inc(job_rd, 1)

            def sm(i):
                return small[:, i, :].rearrange("p (t e) -> p t e", e=E)

            def wide(i):
                return col[:, i, :].unsqueeze(2).to_broadcast([P, QT, E])

            def one_hot(best, src, dst, t0):
                v.tensor_tensor(sm(t0), src, wide(best), ALU.is_equal)
                dve.drain()
                v.tensor_tensor(sm(t0), sm(t0), rev[:, :, :], ALU.mult)
                dve.drain()
                v.tensor_reduce(col[:, 11, :], sm(t0), AX, ALU.max)
                dve.drain()
                v.tensor_tensor(dst, sm(t0), wide(11), ALU.is_equal)

            def gates(n):
                dve.drain()
                wait(dve, scat, 16 * 2 * QT * (n - 1))
                v.tensor_reduce(col[:, 0, :], sm(0), AX, ALU.max)
                dve.drain()
                v.tensor_tensor(sm(1), sm(0), wide(0), ALU.subtract).then_inc(shifted, 1)
                dve.wait_ge(gate_exp, n)
                v.tensor_reduce(col[:, 1, :], sm(2), AX, ALU.add)
                dve.drain()
                v.reciprocal(col[:, 2, :], col[:, 1, :])
                dve.drain()
                v.tensor_tensor(sm(3), sm(2), wide(2), ALU.mult)
                dve.drain()
                v.tensor_reduce(col[:, 3, :], sm(3), AX, ALU.max)
                dve.drain()
                one_hot(3, sm(3), choice[:, 0, :, :], 4)
                dve.drain()
                v.scalar_tensor_tensor(out=sm(5), in0=choice[:, 0, :, :], scalar=-BIG, in1=sm(0),
                                       op0=ALU.mult, op1=ALU.add)
                dve.drain()
                v.tensor_reduce(col[:, 4, :], sm(5), AX, ALU.max)
                dve.drain()
                one_hot(4, sm(5), choice[:, 1, :, :], 6)
                dve.drain()
                v.tensor_tensor(sm(7), sm(3), choice[:, 1, :, :], ALU.mult).then_inc(choice_done, 1)
                dve.drain()
                v.tensor_reduce(col[:, 5, :], sm(7), AX, ALU.add)
                dve.drain()
                v.tensor_tensor(col[:, 6, :], col[:, 3, :], col[:, 5, :], ALU.add)
                dve.drain()
                v.tensor_scalar(col[:, 6, :], col[:, 6, :], 1e-9, None, ALU.add)
                dve.drain()
                v.reciprocal(col[:, 7, :], col[:, 6, :])
                dve.drain()
                v.tensor_tensor(meta[:, :, 0], col[:, 3, :], col[:, 7, :], ALU.mult)
                v.tensor_tensor(meta[:, :, 1], col[:, 5, :], col[:, 7, :], ALU.mult)
                v.tensor_copy(meta[:, :, 2].bitcast(I32), idf[:, :])
                dve.drain()
                v.tensor_scalar(idf[:, :], idf[:, :], float(T), None, ALU.add)

            def routes(n):
                v.tensor_copy(basis[:, :, 0, :], count[:, :, :])
                for t in range(1, QT):
                    dve.drain()
                    v.tensor_tensor(basis[:, :, t, :], basis[:, :, t - 1, :], prefix[:, 1, :, t - 1, :], ALU.add)
                dve.drain()
                v.tensor_tensor(count[:, :, :], basis[:, :, QT - 1, :], prefix[:, 1, :, QT - 1, :], ALU.add)
                v.tensor_tensor(prefix[:, 0, :, :, :], prefix[:, 0, :, :, :], basis[:, :, :, :], ALU.add)
                dve.drain()
                v.tensor_tensor(prefix[:, 0, :, :, :], prefix[:, 0, :, :, :], choice[:, :, :, :], ALU.mult)
                dve.drain()
                v.tensor_reduce(basis[:, :, :, 0], prefix[:, 0, :, :, :], AX, ALU.add)
                dve.drain()
                v.tensor_copy(ridx[:, :, :], basis[:, :, :, 0]).then_inc(route, 1)

            def norm_denominators(n):
                dve.wait_ge(den_in, 16 * n)
                v.reciprocal(rden[:, :], den[:, :]).then_inc(den_rd, 1)

            def norm_outputs(n):
                dve.wait_ge(rb_in, 32 * n)
                dve.wait_ge(ot_in, 32 * n)
                for half in range(2):
                    v.tensor_tensor(oN[:, half, :], oT[:, half, :], rb[:, half, :], ALU.mult).then_inc(o_norm, 1)

            dve.wait_ge(empty_st, 48)
            v.memset(Qs[64:96, :, :, :], 0.0)
            v.memset(Ks[64:96, :, :, :], 0.0)
            v.memset(Ks[96:98, :, :, :], 1.0)
            v.memset(V[:, :, :, :], 1.0)
            v.memset(meta[:, :, :], 0.0)
            dve.wait_ge(wload, 16 * 6)
            v.tensor_scalar(mask_f[:, :], mask_u8[:, :], -1.0, BIG, ALU.add, ALU.mult)
            dve.drain()
            v.tensor_scalar(mask_f[:, :], mask_f[:, :], BIG, None, ALU.mult).then_inc(vset, 1)
            v.memset(Qs[64:65, :, :, :], 1.0).then_inc(vset, 1)

            def first_norm(n, j):
                if j == 0:
                    dve.wait_ge(xa_in, 16 * n)
                if j < 2:
                    statistics(xA, ast, mv1, 2 * j)
                    statistics(xA, ast, mv1, 2 * j + 1)
                    if j == 1:
                        finish_statistics(mv1, ln1_stat)
                if j == 2:
                    dve.wait_ge(ln1_rs, n)
                if j >= 2:
                    normalise(xA, xA, mv1, r1, 2 * j - 4)
                    last = normalise(xA, xA, mv1, r1, 2 * j - 3)
                    if j == 3:
                        last.then_inc(ln1, 1)

            def second_norm(n):
                dve.wait_ge(ln2_rs, n)
                for i in range(QT):
                    last = normalise(h2, x1, mv2, r2, i)
                last.then_inc(ln2, 1)

            for j in range(4):
                first_norm(1, j)
            for n, name in enumerate(AHEAD[:-1]):
                job(-1, FIRST, name, n)
            for h in range(LEAD):
                for qt in range(QT):
                    take_max(0, h, qt)
                if h == G - 1:
                    job(-1, FIRST, "R0n", len(AHEAD) - 1)
            for j in range(4):
                first_norm(2, j)

            def body(b, kind):
                names = jobs_of(kind)
                for j in range(STEPS):
                    h = j + LEAD
                    ahead = h < NH or kind != LAST
                    for qt in range(QT):
                        if qt == 3:
                            for name in JOBS.get(j, []):
                                if name in names:
                                    job(b, kind, name)
                        if ahead:
                            take_max(b + h // NH, h % NH, qt)
                    if kind != LAST and j in NORM_STEPS:
                        first_norm(b + 3, NORM_STEPS.index(j))
                    if kind != FIRST:
                        if j == 3:
                            norm_denominators(b)
                        elif j == 7:
                            norm_outputs(b)
                        elif j == 11:
                            second_norm(b)
                        elif j == 13:
                            gates(b)
                        elif j == 15:
                            routes(b)

            batches(dve, body)
            norm_denominators(NB)
            norm_outputs(NB)
            for name in jobs_of(TAIL):
                job(NB, TAIL, name)
                if name == "O1p":
                    second_norm(NB)
                elif name == "Lp":
                    gates(NB)
            routes(NB)

            def e_(i):
                return ex[:, i, :].unsqueeze(1).to_broadcast([P, TILES, E])

            dve.wait_ge(pv_mm, 16 * NB)
            dve.drain()
            v.tensor_tensor(ex[:, 0:2, :], count[:, :, :], base[:, :, :], ALU.subtract)
            dve.drain()
            v.tensor_scalar(ex[:, 2, :], ex[:, 0, :], float(CAP), None, ALU.min)
            dve.drain()
            v.tensor_scalar(ex[:, 3, :], ex[:, 2, :], -1.0, float(CAP), ALU.mult, ALU.add)
            dve.drain()
            v.tensor_tensor(ex[:, 3, :], ex[:, 3, :], ex[:, 1, :], ALU.min)
            dve.drain()
            v.tensor_tensor(ex[:, 4, :], ex[:, 2, :], ex[:, 3, :], ALU.add)
            dve.drain()
            v.tensor_scalar(nint[:, :], ex[:, 4, :], float(P - 1), None, ALU.add)
            dve.drain()
            v.tensor_scalar(nint[:, :], nint[:, :], 7, None, ALU.arith_shift_right)
            dve.drain()
            v.tensor_copy(ex[:, 5, :], nint[:, :])
            v.memset(ex[:, 6, :], 1.0)
            dve.drain()
            v.tensor_tensor_scan(ex[:, 7, :], ex[:, 6, :], ex[:, 5, :], 0.0, ALU.mult, ALU.add)
            dve.drain()
            v.tensor_tensor(ex[:, 8, :], ex[:, 7, :], ex[:, 5, :], ALU.subtract)
            dve.drain()
            wide_t = tio[:, :].unsqueeze(2).to_broadcast([P, TILES, E])
            v.tensor_tensor(big[:, 0, :, :], wide_t, e_(8), ALU.is_ge)
            v.tensor_tensor(big[:, 1, :, :], wide_t, e_(7), ALU.is_ge)
            dve.drain()
            v.tensor_tensor(big[:, 0, :, :], big[:, 0, :, :], big[:, 1, :, :], ALU.subtract)
            dve.drain()
            for i, src in enumerate((e_(8), e_(2), e_(4), eio[:, :].unsqueeze(1).to_broadcast([P, TILES, E]))):
                v.tensor_tensor(big[:, 1, :, :], big[:, 0, :, :], src, ALU.mult)
                dve.drain()
                v.tensor_reduce(tab[:, i, :], big[:, 1, :, :], AX, ALU.add)
                dve.drain()
            first, kept1, kept, which = (tab[:, i, :] for i in range(4))
            v.tensor_copy(expert_i[:, :], which)
            v.tensor_tensor(tab[:, 4, :], tio[:, :], first, ALU.subtract)
            dve.drain()
            v.tensor_scalar(tab[:, 4, :], tab[:, 4, :], float(P), pio[:, :], ALU.mult, ALU.add)
            dve.drain()
            v.tensor_tensor(tab[:, 5, :], tab[:, 4, :], kept1, ALU.is_lt)
            v.tensor_tensor(tab[:, 6, :], tab[:, 4, :], kept, ALU.is_lt)
            v.tensor_scalar(tab[:, 7, :], kept1, -1.0, float(REGION), ALU.mult, ALU.add)
            dve.drain()
            v.tensor_scalar(tab[:, 8, :], tab[:, 5, :], -1.0, 1.0, ALU.mult, ALU.add)
            v.tensor_copy(pick[:, :, 0], tab[:, 5, :])
            dve.drain()
            v.tensor_copy(pick[:, :, 1], tab[:, 8, :])
            v.tensor_tensor(tab[:, 7, :], tab[:, 7, :], tab[:, 8, :], ALU.mult)
            dve.drain()
            v.tensor_tensor(tab[:, 4, :], tab[:, 4, :], tab[:, 7, :], ALU.add)
            dve.drain()
            v.scalar_tensor_tensor(out=tab[:, 4, :], in0=which, scalar=float(2 * REGION), in1=tab[:, 4, :],
                                   op0=ALU.mult, op1=ALU.add)
            dve.drain()
            v.tensor_scalar(tab[:, 4, :], tab[:, 4, :], -float(NREG * REGION), None, ALU.add)
            dve.drain()
            v.tensor_tensor(tab[:, 4, :], tab[:, 4, :], tab[:, 6, :], ALU.mult)
            dve.drain()
            v.tensor_scalar(rows_i[:, 0:TILES], tab[:, 4, :], float(NREG * REGION), None, ALU.add)
            v.memset(rows_i[:, TILES:TILES + RING], NREG * REGION)
            dve.drain()
            v.tensor_copy(ex[:, 9, :], ex[:, 0, :]).then_inc(tiles_done, 1)

            def bias(t, half, e):
                dve.wait_ge(h_mm, 2 * t + half + 1)
                wait(dve, h_g, 2 * t - 1 + half)
                v.tensor_tensor(hb[:, half * 512:(half + 1) * 512], psT[:, half, :],
                                b1r[:, bass.ds(e, 1), half * 512:(half + 1) * 512], ALU.add).then_inc(h_b, 1)

            def expert_of(t):
                return dve.value_load(expert_i[0:1, bass.ds(t, 1)], min_val=0, max_val=E - 1)

            def expert_step(t, u, r):
                more = not isinstance(t, int) or t + 1 < TILES
                dve.wait_ge(g_meta[u], 16 * (r + 1))
                v.tensor_tensor(wpair[:, u % 2, :], meta_in[:, u, 0:2], pick[:, bass.ds(t, 1), :], ALU.mult)
                if more:
                    e1 = expert_of(t + 1)
                    bias(t + 1, 0, e1)
                dve.drain()
                v.tensor_reduce(wcol[:, u % 2:u % 2 + 1], wpair[:, u % 2, :], AX, ALU.add)
                dve.wait_ge(h_tr, 2 * t + 2)
                wait(dve, y_mm, t)
                v.tensor_copy(hT[:, 4:8, :], psT[:, 3, :].rearrange("p (k n) -> p k n", k=4)).then_inc(h_trd, 1)
                if more:
                    bias(t + 1, 1, e1)
                e = expert_of(t)
                dve.wait_ge(y_mm, t + 1)
                v.tensor_tensor(y0[:, :], psMax[:, u % 2, 0:D], b2r[:, bass.ds(e, 1), :], ALU.add)
                dve.drain()
                wait(dve, added, 16 * (t - 1))
                v.tensor_scalar(y[:, u % 2, :], y0[:, :], wcol[:, u % 2:u % 2 + 1], None, ALU.mult).then_inc(y_done, 1)

            dve.wait_ge(tiles_done, 1)
            dve.wait_ge(bload, 32)
            e0 = expert_of(0)
            bias(0, 0, e0)
            bias(0, 1, e0)
            tiles(dve, expert_step)

        @block.gpsimd
        def _(pool):
            g = nc.gpsimd
            g.memset(fill0[:, :, :], 0.0)
            g.memset(rb[:, :, :], 0.0).then_inc(tio_done, 1)
            pool.wait_ge(tio_done, 1)
            g.memset(fill0[:, :, 2:3].bitcast(I32), NTOK).then_inc(tio_done, 1)
            pool.wait_ge(tio_done, 2)
            pool.dma_start(table[0:NREG * REGION].rearrange("(p r) c -> p r c", p=P), fill0[:, :, :]).then_inc(empty_st, 16)
            pool.dma_start(table[NREG * REGION:], fill0[:, 0, :]).then_inc(empty_st, 16)
            pool.dma_start(h2d[NTOK:], rb[:, 0, 0:D]).then_inc(empty_st, 16)
            g.memset(ident[:, :], 0.0)
            g.memset(upper[:, :], 1.0)
            g.memset(ones[:, :], 1.0)
            g.memset(mhalf[:, :], -0.5)
            g.iota(rev[:, :, :], [[0, QT], [-1, E]], base=E, channel_multiplier=0, allow_small_or_imprecise_dtypes=True)
            g.iota(idf[:, :], [[P, QT]], base=0, channel_multiplier=1, allow_small_or_imprecise_dtypes=True)
            g.iota(base[:, :, :], [[REGION, 2], [2 * REGION, E]], base=0, channel_multiplier=0,
                   allow_small_or_imprecise_dtypes=True)
            g.iota(count[:, :, :], [[REGION, 2], [2 * REGION, E]], base=0, channel_multiplier=0,
                   allow_small_or_imprecise_dtypes=True)
            g.iota(tio[:, :], [[1, TILES]], base=0, channel_multiplier=0, allow_small_or_imprecise_dtypes=True)
            g.iota(eio[:, :], [[1, E]], base=0, channel_multiplier=0, allow_small_or_imprecise_dtypes=True)
            g.iota(pio[:, :], [[0, 1]], base=0, channel_multiplier=1,
                   allow_small_or_imprecise_dtypes=True).then_inc(tio_done, 1)
            pool.wait_ge(tio_done, 3)
            g.affine_select(out=ident[:, :], in_=ident[:, :], compare_op=ALU.not_equal, fill=1.0, base=0,
                            pattern=[[-1, P]], channel_multiplier=1)
            g.affine_select(out=upper[:, :], in_=upper[:, :], compare_op=ALU.is_gt, fill=0.0, base=0,
                            pattern=[[1, P]], channel_multiplier=-1).then_inc(setup, 1)

            def inverse_root(mv, rs, stat, done, n):
                pool.wait_ge(stat, n)
                g.tensor_tensor(rs[:, :], mv[:, :, 1], mhalf[:, :], ALU.pow).then_inc(done, 1)

            def keep(n):
                pool.wait_ge(ln2, n)
                pool.dma_start(out[n - 1].rearrange("(t p) d -> p t d", p=P), x1[:, :, :]).then_inc(x1_st, 16)
                pool.dma_start(h2d[0:NTOK].rearrange("(b t p) d -> b p t d", b=NB, p=P)[n - 1], h2[:, :, :]).then_inc(x1_st, 16)

            def scatter(n):
                pool.wait_ge(route, n)
                pool.sem_inc(pool_step, 1)
                for k in range(2):
                    for t in range(QT):
                        g.indirect_dma_start(table[:, :], bass.IndirectOffsetOnAxis(
                            ap=ridx[:, k, t:t + 1].bitcast(U32), axis=0), meta[:, t, :], None).then_inc(scat, 16)

            inverse_root(mv1, r1, ln1_stat, ln1_rs, 1)
            inverse_root(mv1, r1, ln1_stat, ln1_rs, 2)
            pool.wait_ge(empty_st, 48)

            def body(b, kind):
                if kind != LAST:
                    inverse_root(mv1, r1, ln1_stat, ln1_rs, b + 3)
                if kind != FIRST:
                    inverse_root(mv2, r2, ln2_stat, ln2_rs, b)
                    keep(b)
                    scatter(b)

            batches(pool, body)
            inverse_root(mv2, r2, ln2_stat, ln2_rs, NB)
            keep(NB)
            scatter(NB)

            def gather_meta(t, u):
                g.tensor_copy(rowidx[:, u:u + 1], rows_i[:, bass.ds(t, 1)]).then_inc(rix, 1)
                pool.wait_ge(rix, t + 1)
                pool.sem_inc(pool_step, 1)
                g.indirect_dma_start(meta_in[:, u, :], None, table[:, :], bass.IndirectOffsetOnAxis(
                    ap=rowidx[:, u:u + 1].bitcast(U32), axis=0)).then_inc(g_meta[u], 16)

            def gather_tokens(t, u, r):
                pool.wait_ge(g_meta[u], 16 * (r + 1))
                wait(pool, x_tr, t - RING + 1)
                pool.sem_inc(pool_step, 1)
                g.indirect_dma_start(X[:, u, :], None, h2d[:, :], bass.IndirectOffsetOnAxis(
                    ap=meta_in[:, u, 2:3].bitcast(U32), axis=0)).then_inc(g_x[u], 16)

            pool.wait_ge(tiles_done, 1)
            pool.wait_ge(scat, 16 * 2 * QT * NB)
            pool.wait_ge(x1_st, 32 * NB)
            for t in range(RING):
                gather_meta(t, t)
            for t in range(RING - 1):
                gather_tokens(t, t, 0)
            out_rows = out.rearrange("b t d -> (b t) d")

            def expert_step(t, u, r):
                if not isinstance(t, int) or t + 3 < TILES:
                    gather_tokens(t + 3, (u + 3) % RING, r + (u + 3) // RING)
                pool.wait_ge(y_done, t + 1)
                pool.sem_inc(pool_step, 1)
                g.indirect_dma_start(out_rows, bass.IndirectOffsetOnAxis(ap=meta_in[:, u, 2:3].bitcast(U32), axis=0),
                                     y[:, u % 2, :], None, compute_op=ALU.add, bounds_check=NTOK - 1,
                                     oob_is_err=False).then_inc(added, 16)
                pool.wait_ge(added, 16 * (t + 1))
                if not isinstance(t, int) or t + RING < TILES:
                    gather_meta(t + RING, u)

            tiles(pool, expert_step)


def kernel(x, ctx_1024, mask_Bx1x1xS2_bf1, L0_xattn_Wq, L0_xattn_Wk, L0_xattn_Wv, L0_xattn_Wo,
           L0_ffn_Wg, L0_ffn_W1, L0_ffn_b1, L0_ffn_W2, L0_ffn_b2):
    import numpy as np
    import concourse.bacc as bacc
    from concourse.bass_utils import run_bass_kernel_spmd

    arrays = {
        "x": np.asarray(x),
        "ctxT": np.ascontiguousarray(np.asarray(ctx_1024).transpose(0, 2, 1)),
        "mask": np.asarray(mask_Bx1x1xS2_bf1).reshape(NB, T).view(np.uint8),
        "WqT": np.ascontiguousarray(np.asarray(L0_xattn_Wq).T),
        "WkT": np.ascontiguousarray(np.asarray(L0_xattn_Wk).T),
        "WvT": np.ascontiguousarray(np.asarray(L0_xattn_Wv).T),
        "WoT": np.ascontiguousarray(np.asarray(L0_xattn_Wo).T),
        "Wg": np.asarray(L0_ffn_Wg), "W1": np.asarray(L0_ffn_W1),
        "b1": np.asarray(L0_ffn_b1).reshape(-1), "W2": np.asarray(L0_ffn_W2),
        "b2": np.asarray(L0_ffn_b2).reshape(-1),
    }
    nc = bacc.Bacc("TRN2", target_bir_lowering=False, num_devices=1)
    args = [nc.dram_tensor(n, a.shape, mybir.dt.from_np(a.dtype), kind="ExternalInput").ap()
            for n, a in arrays.items()]
    out = nc.dram_tensor("out", (NB, T, D), F32, kind="ExternalOutput").ap()
    build(nc, *args, out)
    r = run_bass_kernel_spmd(nc, [arrays], core_ids=[0])
    return r.results[0]["out"]
```

```python
from contextlib import ExitStack

import concourse.bass as bass
from concourse import mybir

F32 = mybir.dt.float32
F32R = mybir.dt.float32r
I32 = mybir.dt.int32
U32 = mybir.dt.uint32
U8 = mybir.dt.uint8
ALU = mybir.AluOpType
ACT = mybir.ActivationFunctionType
AX = mybir.AxisListType.X

P = 128
NB, T, D = 8, 512, 256
NH, DH = 16, 16
G = 4
NG = NH // G
QT = T // P
KD = D // P
E, FF = 8, 1024
KF = FF // P
CAP = 2 * 2 * NB * T // E
REGION = NB * T
NREG = 2 * E
NTOK = NB * T
TILES = (2 * NTOK - E) // P + E
LEAD = 6
STEPS = NG * QT
SCALE = DH ** -0.5
EPS = 1e-5
BIG = 3e38
LEFT_OUT = 2.0 ** 100
RING = 6
HALF = KD * FF
CHUNK = HALF // 2
SLOTS = 4
SROWS, TROWS = 96, 98

JOBS = [(["T0n"], ["T1n"]), ([], ["V1"]), (["R1"], []), ([], ["Q0n"]), ([], ["K0n"]), ([], ["K1n"]), (["R2"], ["Q1n"]),
        ([], ["O0p"]), ([], ["O1p"]), ([], ["V0n"]), (["R3"], []), (["U0p"], ["U1p"]), (["Lp"], []), ([], ["R0n"]),
        ([], []), (["Pp"], [])]
AHEAD = ["T0n", "T1n", "Q0n", "K0n", "K1n", "Q1n", "V0n", "R0n"]
NORM_SLOTS = [(4, 0), (4, 2), (5, 0), (5, 2)]
H2_SLOTS = [(9, 2), (9, 3), (10, 0), (10, 1)]
GATE_SLOTS = [(12, 3), (13, 2), (13, 3), (14, 0), (14, 1), (14, 2), (14, 3), (15, 0)]
SPLITS = [(2, 1), (2, 3), (6, 0), (6, 2), (10, 1), (10, 3), (13, 1), (13, 3)]
FIRST, MID, LAST, TAIL = range(4)


def jobs_of(kind):
    if kind == TAIL:
        return ["O0p", "O1p", "U0p", "U1p", "Lp", "Pp"]
    return [n for step in JOBS for half in step for n in half
            if not (kind == FIRST and n[-1] == "p") and not (kind == LAST and n[-1] == "n")]


PER = len(jobs_of(MID))


def number(b, kind, name):
    before = len(AHEAD) + (0 if kind == FIRST else len(jobs_of(FIRST)) - PER)
    if kind == TAIL:
        return before + (NB - 1) * PER + len(jobs_of(LAST)) + jobs_of(kind).index(name)
    return before + b * PER + jobs_of(kind).index(name)


def build(nc, x, ctxT, mask, WqT, WkT, WvT, WoT, Wg, W1, b1, W2, b2, out):
    with ExitStack() as ctx:
        def sem(name):
            return ctx.enter_context(nc.semaphore(name))

        place = [nc.sbuf_base + (-nc.sbuf_base) % 64]
        ctx.enter_context(nc.sbuf_tensor("arena", [P, (nc.sbuf_usable_end - place[0]) // 4 - 16], F32))

        def at(name, shape, dt=F32):
            n = 1 if dt == U8 else 4
            for s in shape[1:]:
                n *= s
            t = nc.alloc_sbuf_tensor_at(name, shape, dt, offset=place[0])
            place[0] += n + (-n) % 32
            return t

        b1r = at("b1r", [P, E, FF])
        raw, whi, wlo = (nc.alloc_sbuf_tensor_at(name, [P, 2, CHUNK], F32, offset=place[0] - 4 * E * FF + 8 * CHUNK * i)
                         for i, name in enumerate(("raw", "whi", "wlo")))
        b2r = at("b2r", [P, E, D])
        ident = at("ident", [P, P])
        upper = at("upper", [P, P])
        ones = at("ones", [P, P])
        rev = at("rev", [P, QT, E])
        count = at("count", [P, 2, E])
        wg_sb = at("wg_sb", [P, KD, E])
        mhalf = at("mhalf", [P, QT])
        expert_i = at("expert_i", [P, TILES], I32)
        after_i = at("after_i", [P, E], I32)
        rows_i = at("rows_i", [P, TILES + RING], I32)
        pick = at("pick", [P, TILES, 2])
        base = at("base", [P, 2, E])
        tio = at("tio", [P, TILES])
        pio = at("pio", [P, 1])
        ex = at("ex", [P, 10, E])
        nint = at("nint", [P, E], I32)
        shared = place[0]
        X = at("X", [P, RING, D])
        meta_in = at("meta_in", [P, RING, 4])
        rowidx = at("rowidx", [P, RING], I32)
        XT = at("XT", [P, 2, KD, P])
        hb = at("hb", [P, FF])
        hg = at("hg", [P, FF])
        hT = at("hT", [P, 2, KF, P])
        y = at("y", [P, 2, D])
        y0 = at("y0", [P, D])
        wpair = at("wpair", [P, 2, 2])
        wcol = at("wcol", [P, 2])
        ffn_end = place[0]
        place[0] = shared
        wo_sb = at("wo_sb", [P, KD, D])
        big = nc.alloc_sbuf_tensor_at("big", [P, 2, TILES, E], F32, offset=place[0])
        tab = nc.alloc_sbuf_tensor_at("tab", [P, 10, TILES], F32, offset=place[0] + 4 * 2 * TILES * E)
        oN = at("oN", [P, 2, T])
        oT = at("oT", [P, 2, T])
        rb = at("rb", [P, 2, T])
        mask_f = nc.alloc_sbuf_tensor_at("mask_f", [NB, T], F32, offset=place[0])
        mask_u8 = nc.alloc_sbuf_tensor_at("mask_u8", [NB, T], U8, offset=place[0] + 4 * T)
        xR = at("xR", [P, QT, D])
        x1 = at("x1", [P, QT, D])
        h2 = at("h2", [P, QT, D])
        fill0 = nc.alloc_sbuf_tensor_at("fill0", [P, NREG * REGION // P, 4], F32, offset=place[0] - 8 * QT * D)
        h2T = at("h2T", [P, KD, T])
        den = at("den", [P, NH * T // P])
        rden = at("rden", [P, NH * T // P])
        meta = at("meta", [P, QT, 4])
        ridx = at("ridx", [P, 2, QT], I32)
        small = at("small", [P, 16, QT * E])
        choice = at("choice", [P, 2, QT, E])
        col = at("col", [P, 12, QT])
        idf = at("idf", [P, QT])
        bst = at("bst", [P, QT, 6])
        mv2 = at("mv2", [P, QT, 2])
        r2 = at("r2", [P, QT])
        prefix = at("prefix", [P, 2, 2, QT, E])
        basis = at("basis", [P, 2, QT, E])
        place[0] = max(place[0], ffn_end)
        upto = place[0]
        Ws = at("Ws", [P, SLOTS, 2, 2 * HALF])
        weights_end = place[0]
        place[0] = upto
        Qs = at("Qs", [TROWS, NG, G, T])
        Ks = at("Ks", [TROWS, NG, G, T])
        Qhi = at("Qhi", [P, 2, T])
        Qlo = at("Qlo", [P, 2, T])
        Khi = at("Khi", [P, 2, T])
        Klo = at("Klo", [P, 2, T])
        xA = at("xA", [P, QT, D])
        xnT = at("xnT", [P, KD, T])
        cT = at("cT", [P, KD, T])
        wq_sb = at("wq_sb", [P, KD, D])
        wk_sb = at("wk_sb", [P, KD, D])
        probs = at("probs", [P, 2, G, T])
        V = at("V", [P, QT, NH, 2 * DH])
        wv_sb = at("wv_sb", [P, KD, D])
        oraw = at("oraw", [P, 2, T])
        negmax = at("negmax", [P, 2, G * QT])
        mhi = at("mhi", [G * QT, 2, P])
        mlo = at("mlo", [G * QT, 2, P])
        ast = at("ast", [P, QT, 6])
        mv1 = at("mv1", [P, QT, 2])
        r1 = at("r1", [P, QT])
        attention_end = place[0]
        assert max(weights_end, attention_end) <= nc.sbuf_usable_end - 64

        psMax = ctx.enter_context(nc.psum_tensor("psMax", [P, 4, 512], F32))
        psT = ctx.enter_context(nc.psum_tensor("psT", [P, 2, 512], F32))
        psO = ctx.enter_context(nc.psum_tensor("psO", [P, 512], F32))
        psM = ctx.enter_context(nc.psum_tensor("psM", [P, 512], F32))

        qd = nc.dram_tensor("qd", [3 * DH + 1, NH, T], F32, kind="Internal").ap()
        kd = nc.dram_tensor("kd", [NB, 2 * DH + 1, NH, T], F32, kind="Internal").ap()
        od = nc.dram_tensor("od", [NH, 2 * DH, T], F32, kind="Internal").ap()
        rdend = nc.dram_tensor("rdend", [NH, T], F32, kind="Internal").ap()
        table = nc.dram_tensor("table", [NREG * REGION + P, 4], F32, kind="Internal").ap()
        wparts = nc.dram_tensor("wparts", [E, 2, P, 2 * HALF], F32, kind="Internal").ap()
        h2d = nc.dram_tensor("h2d", [NTOK + P, D], F32, kind="Internal").ap()

        pool_step = sem("pool_step")
        sp_step = sem("sp_step")
        wload = sem("wload")
        bload = sem("bload")
        setup = sem("setup")
        vset = sem("vset")
        maskst = sem("maskst")
        xa_in = sem("xa_in")
        ct_in = sem("ct_in")
        xr_in = sem("xr_in")
        ln1_stat = sem("ln1_stat")
        ln1_rs = sem("ln1_rs")
        ln1 = sem("ln1")
        job_mm = sem("job_mm")
        job_rd = sem("job_rd")
        hi_done = sem("hi_done")
        filled = [sem(f"filled{g}") for g in range(NG)]
        mrow = [sem(f"mrow{g}") for g in range(NG)]
        smax_mm = sem("smax_mm")
        max_rd = sem("max_rd")
        st_mm = sem("st_mm")
        exp_rd = sem("exp_rd")
        pv_mm = sem("pv_mm")
        o_copy = sem("o_copy")
        o_out = [sem(f"o_out{i}") for i in range(2)]
        ot_in = sem("ot_in")
        stored = [sem(f"stored{i}") for i in range(2)]
        den_in = sem("den_in")
        den_rd = sem("den_rd")
        den_st = sem("den_st")
        rb_in = sem("rb_in")
        o_norm = sem("o_norm")
        x1_done = sem("x1_done")
        ln2_stat = sem("ln2_stat")
        ln2_rs = sem("ln2_rs")
        ln2 = sem("ln2")
        x1_st = sem("x1_st")
        shifted = sem("shifted")
        gate_exp = sem("gate_exp")
        choice_done = sem("choice_done")
        route = sem("route")
        empty_st = sem("empty_st")
        scat = sem("scat")
        tiles_done = sem("tiles_done")
        w_raw = [sem(f"w_raw{i}") for i in range(2)]
        w_hi = sem("w_hi")
        w_lo = sem("w_lo")
        w_st = [sem(f"w_st{i}") for i in range(2)]
        w_in = sem("w_in")
        w_ready = sem("w_ready")
        tio_done = sem("tio_done")
        rix = sem("rix")
        g_meta = [sem(f"g_meta{i}") for i in range(RING)]
        g_x = [sem(f"g_x{i}") for i in range(RING)]
        x_tr = sem("x_tr")
        x_hi = sem("x_hi")
        x_lo = sem("x_lo")
        h_mm = sem("h_mm")
        h_b = sem("h_b")
        h_g = sem("h_g")
        h_tr = sem("h_tr")
        h_hi = sem("h_hi")
        h_lo = sem("h_lo")
        y_mm = sem("y_mm")
        y_done = sem("y_done")
        added = sem("added")

        def wait(eng, s, value):
            if not isinstance(value, int) or value > 0:
                eng.wait_ge(s, value)

        def batches(eng, body):
            body(0, FIRST)
            body(1, MID)
            with eng.Fori(2, NB - 1) as b:
                body(b, MID)
            body(NB - 1, LAST)

        def tiles(eng, body):
            rounds = (TILES - 4) // RING
            body(0, 0, 0, True)
            body(1, 1, 0, False)
            with eng.Fori(0, rounds) as i:
                for u in range(2, RING + 2):
                    body(i * RING + u, u % RING, i + u // RING, u == 2)
            for t in range(rounds * RING + 2, TILES):
                body(t, t % RING, t // RING, t == rounds * RING + 2)

        FILLS = 16 * 4
        STORES = 16 * 5
        ROWS4 = (lambda b: x[b].rearrange("(t p) d -> p t d", p=P))

        block = ctx.enter_context(nc.Block())

        @block.sync
        def _(sp):
            def store_parts(b, half):
                hs = slice(half * 8, half * 8 + 8)

                def put(dst, r, part):
                    sp.dma_start(dst[r:r + DH, hs, :].rearrange("d h n -> h d n"),
                                 part[:, half, :]).then_inc(stored[half], 16)
                put(qd, 0, Qhi)
                put(qd, DH, Qlo)
                put(qd, 2 * DH, Qhi)
                put(kd[b], 0, Khi)
                put(kd[b], DH, Klo)

            def fill(b, g):
                sp.sem_inc(sp_step, 1)
                sp.wait_ge(stored[g // 2], STORES * (b + 1))
                hs = slice(g * G, g * G + G)
                for r, n, src in ((0, 32, qd[0:32, hs, :]), (32, 33, qd[16:49, hs, :])):
                    sp.dma_start(Qs[r:r + n, g, :, :], src).then_inc(filled[g], 16)
                for r, n in ((0, 32), (32, 33)):
                    sp.dma_start(Ks[r:r + n, g, :, :], kd[b][0:n, hs, :]).then_inc(filled[g], 16)

            def store_out(g):
                sp.dma_start(od[g * G:g * G + G, :, :].rearrange("h r n -> (h r) n"),
                             oraw[:, g % 2, :]).then_inc(o_out[g % 2], 16)

            def put_max(g):
                i = g % 2
                sp.dma_start(Qs[96:97, g, :, :], mhi[:, i, :]).then_inc(mrow[g], 16)
                sp.dma_start(Qs[97:98, g, :, :], mlo[:, i, :]).then_inc(mrow[g], 16)

            def out_load(n):
                sp.wait_ge(o_out[0], 32 * n)
                sp.wait_ge(o_out[1], 32 * n)
                sp.dma_start(den[:, :], od[:, DH, :].rearrange("h (a n) -> h a n", n=NH * T // P)).then_inc(den_in, 16)
                wait(sp, o_norm, 2 * (n - 1))
                for half in range(2):
                    sp.dma_start(oT[:, half, :], od[half * 8:half * 8 + 8, 0:DH, :]).then_inc(ot_in, 16)

            def den_back(n):
                sp.wait_ge(den_rd, n)
                sp.dma_start(rdend.rearrange("h (a n) -> h a n", n=NH * T // P), rden[:, :]).then_inc(den_st, 16)
                sp.wait_ge(den_st, 16 * n)
                for half in range(2):
                    sp.dma_start(rb[:, half, :], rdend[half * 8:half * 8 + 8].unsqueeze(1).to_broadcast(
                        [8, DH, T])).then_inc(rb_in, 16)

            def load_quarters(slots, quarters):
                for e in slots:
                    for q in quarters:
                        i = q % 2
                        sp.dma_start(Ws[:, e, q // 2, i * HALF:(i + 1) * HALF],
                                     wparts[e, q // 2, :, i * HALF:(i + 1) * HALF]).then_inc(w_in, 16)

            def chunk_of(e, c):
                if c < 2:
                    return W1[e].rearrange("(k p) f -> k p f", p=P)[c]
                return W2[e].rearrange("(i k p) n -> i p k n", i=2, p=P)[c - 2]

            def load_chunk(e, c):
                sp.dma_start(raw[:, c % 2, :], chunk_of(e, c)).then_inc(w_raw[c % 2], 16)

            def store_chunk(e, c):
                sp.wait_ge(w_lo, 4 * e + c + 1)
                for part, src in enumerate((whi, wlo)):
                    sp.dma_start(wparts[e, part, :, c * CHUNK:(c + 1) * CHUNK], src[:, c % 2, :]).then_inc(w_st[c % 2], 16)

            sp.dma_start(xA[:, :, :], ROWS4(0)).then_inc(xa_in, 16)
            sp.dma_start(mask_u8[:, :], mask).then_inc(wload, 16)
            sp.dma_start(wq_sb[:, :, :], WqT.rearrange("(k p) n -> p k n", p=P)).then_inc(wload, 16)
            sp.dma_start(cT[:, :, :], ctxT[0].rearrange("(k p) n -> p k n", p=P)).then_inc(ct_in, 16)
            for dst, src in ((wk_sb, WkT), (wv_sb, WvT), (wo_sb, WoT), (wg_sb, Wg)):
                sp.dma_start(dst[:, :, :], src.rearrange("(k p) n -> p k n", p=P)).then_inc(wload, 16)
            sp.wait_ge(setup, 1)
            sp.dma_start(qd[3 * DH].rearrange("h (a n) -> (h a) n", n=NH * T // P),
                         ones[:, 0:NH * T // P]).then_inc(maskst, 16)
            sp.wait_ge(vset, 1)
            sp.dma_start(kd[:, 2 * DH, :, :], mask_f[:, :].unsqueeze(1).to_broadcast([NB, NH, T])).then_inc(maskst, 16)
            sp.wait_ge(job_rd, 2)
            sp.dma_start(xA[:, :, :], ROWS4(1)).then_inc(xa_in, 16)
            load_chunk(0, 0)
            load_chunk(0, 1)
            sp.wait_ge(job_rd, 4)
            store_parts(0, 0)
            sp.wait_ge(maskst, 32)
            sp.wait_ge(vset, 3)
            fill(0, 0)
            sp.wait_ge(job_rd, 6)
            store_parts(0, 1)
            for g in range(1, NG):
                fill(0, g)
            sp.wait_ge(job_rd, 8)
            put_max(0)

            def body(b, kind):
                num = lambda name: number(b, kind, name)
                if kind != FIRST:
                    sp.wait_ge(o_copy, 4 * b)
                    store_out(3)
                if kind != LAST:
                    sp.wait_ge(job_rd, num("T1n") + 1)
                    sp.dma_start(xA[:, :, :], ROWS4((b + 2) % NB)).then_inc(xa_in, 16)
                if kind != FIRST:
                    out_load(b)
                    sp.wait_ge(st_mm, 64 * b)
                    fill(b, 3)
                if kind != LAST:
                    sp.wait_ge(job_rd, num("V1") + 1)
                    sp.dma_start(cT[:, :, :], ctxT[b + 1].rearrange("(k p) n -> p k n", p=P)).then_inc(ct_in, 16)
                sp.wait_ge(job_rd, num("R1") + 1)
                put_max(1)
                if kind != FIRST:
                    wait(sp, x1_done, 2 * (b - 1))
                    sp.dma_start(xR[:, :, :], ROWS4(b - 1)).then_inc(xr_in, 16)
                    den_back(b)
                    store_chunk(b - 1, 3)
                    load_chunk(b, 1)
                    sp.wait_ge(ot_in, 32 * b)
                    sp.sem_inc(sp_step, 1)
                if kind == LAST:
                    sp.wait_ge(stored[0], STORES * NB)
                    sp.wait_ge(stored[1], STORES * NB)
                    for i in range(2):
                        sp.wait_ge(w_st[i], 32 * 2 * SLOTS)
                    load_quarters((2,), (0, 1))
                sp.wait_ge(o_copy, 4 * b + 1)
                store_out(0)
                if kind != LAST:
                    sp.wait_ge(job_rd, num("K0n") + 1)
                    sp.sem_inc(sp_step, 1)
                    sp.wait_ge(filled[1], FILLS * (b + 1))
                    store_parts(b + 1, 0)
                sp.wait_ge(job_rd, num("R2") + 1)
                put_max(2)
                store_chunk(b, 0)
                load_chunk(b, 2)
                if kind == LAST:
                    sp.wait_ge(ln1, NB + 1)
                    load_quarters((2,), (2, 3))
                    sp.wait_ge(st_mm, 64 * b + 16)
                    load_quarters((0, 1), (0,))
                if kind != LAST:
                    sp.wait_ge(st_mm, 64 * b + 16)
                    fill(b + 1, 0)
                    sp.wait_ge(job_rd, num("Q1n") + 1)
                    sp.wait_ge(filled[3], FILLS * (b + 1))
                    store_parts(b + 1, 1)
                sp.wait_ge(o_copy, 4 * b + 2)
                store_out(1)
                if kind != LAST:
                    sp.wait_ge(st_mm, 64 * b + 32)
                    fill(b + 1, 1)
                sp.wait_ge(job_rd, num("R3") + 1)
                put_max(3)
                store_chunk(b, 1)
                load_chunk(b, 3)
                if kind == LAST:
                    sp.wait_ge(st_mm, 64 * b + 32)
                    load_quarters((0, 1), (1,))
                if kind != LAST:
                    sp.wait_ge(st_mm, 64 * b + 48)
                    fill(b + 1, 2)
                sp.wait_ge(o_copy, 4 * b + 3)
                store_out(2)
                if kind == LAST:
                    sp.wait_ge(st_mm, 64 * b + 48)
                    load_quarters((0, 1), (2,))
                if kind != LAST:
                    sp.wait_ge(job_rd, num("R0n") + 1)
                    put_max(0)
                store_chunk(b, 2)
                if kind != LAST:
                    load_chunk(b + 1, 0)

            batches(sp, body)
            sp.wait_ge(o_copy, 4 * NB)
            store_out(3)
            out_load(NB)
            store_chunk(NB - 1, 3)
            sp.wait_ge(x1_done, 2 * (NB - 1))
            sp.dma_start(xR[:, :, :], ROWS4(NB - 1)).then_inc(xr_in, 16)
            den_back(NB)
            sp.wait_ge(pv_mm, 16 * NB)
            load_quarters((0, 1), (3,))
            load_quarters((3,), (0, 1, 2))
            for g in range(NG):
                sp.wait_ge(mrow[g], 32 * NB)
            load_quarters((3,), (3,))
            sp.wait_ge(w_in, 16 * 4 * SLOTS)
            sp.sem_inc(w_ready, SLOTS)
            for i in range(2):
                sp.wait_ge(w_st[i], 32 * 2 * E)
            sp.wait_ge(tiles_done, 1)
            for e in range(SLOTS, E):
                after = sp.value_load(after_i[0:1, e - SLOTS:e - SLOTS + 1], min_val=1, max_val=TILES + 1)
                sp.wait_ge(y_mm, after)
                sp.sem_inc(sp_step, 1)
                for i in range(8):
                    part, cols = i // 4, slice(i % 4 * CHUNK, (i % 4 + 1) * CHUNK)
                    sp.dma_start(Ws[:, e % SLOTS, part, cols], wparts[e, part, :, cols]).then_inc(w_in, 16)
                    sp.wait_ge(w_in, 16 * (4 * SLOTS + 8 * (e - SLOTS) + i + 1))
                sp.sem_inc(w_ready, 1)

        @block.tensor
        def _(pe):
            def scores_max(b, h, qt):
                g, hh = h // G, h % G
                if qt == 0 and hh == 0:
                    pe.wait_ge(filled[g], FILLS * (b + 1))
                wait(pe, max_rd, 4 * (NH * b + h) + qt - 3)
                nc.tensor.matmul(psMax[:, qt, :], Qs[0:SROWS, g, hh, qt * P:(qt + 1) * P].bitcast(F32R),
                                 Ks[0:SROWS, g, hh, :].bitcast(F32R), start=True, stop=True).then_inc(smax_mm, 1)

            def scores_t(b, j, hh):
                g, kt = j // QT, j % QT
                if kt == 0 and hh == 0:
                    pe.wait_ge(mrow[g], 32 * (b + 1))
                wait(pe, exp_rd, G * (STEPS * b + j) + hh - 1)
                nc.tensor.matmul(psT[:, hh % 2, :], Ks[0:TROWS, g, hh, kt * P:(kt + 1) * P].bitcast(F32R),
                                 Qs[0:TROWS, g, hh, :].bitcast(F32R), start=True, stop=True).then_inc(st_mm, 1)

            def values(b, j):
                g, kt = j // QT, j % QT
                pe.wait_ge(exp_rd, G * (STEPS * b + j) + G)
                if kt == 0:
                    wait(pe, o_copy, NG * b + g)
                for hh in range(G):
                    last = nc.tensor.matmul(psO[32 * hh:32 * hh + 32, :], V[:, kt, g * G + hh, :],
                                            probs[:, j % 2, hh, :], start=(kt == 0), stop=(kt == QT - 1))
                last.then_inc(pv_mm, 1)

            def job(b, kind, name, n=None):
                n = number(b, kind, name) if n is None else n
                wait(pe, job_rd, n)
                what = name[0]
                if what == "T":
                    k = int(name[1])
                    if k == 0:
                        pe.wait_ge(ln1, b + 2)
                    for i in range(QT):
                        last = nc.tensor.transpose(psM[:, i * P:(i + 1) * P], xA[:, i, k * P:(k + 1) * P], ident[:, :])
                elif what in "QK":
                    half = int(name[1])
                    w, src = (wq_sb, xnT) if what == "Q" else (wk_sb, cT)
                    if name[:2] == "K0":
                        pe.wait_ge(ct_in, 16 * (b + 2))
                    for k in range(KD):
                        last = nc.tensor.matmul(psM[:, :], w[:, k, half * P:(half + 1) * P], src[:, k, :],
                                                start=(k == 0), stop=(k == KD - 1))
                elif what == "V":
                    half = int(name[1])
                    for kt in range(QT):
                        for k in range(KD):
                            last = nc.tensor.matmul(psM[:, kt * P:(kt + 1) * P], cT[:, k, kt * P:(kt + 1) * P],
                                                    wv_sb[:, k, half * P:(half + 1) * P],
                                                    start=(k == 0), stop=(k == KD - 1))
                elif what == "R":
                    g = int(name[1])
                    nb = b + 1 if name[-1] == "n" else b
                    pe.wait_ge(max_rd, 4 * (NH * nb + G * g + G))
                    last = nc.tensor.transpose(psM[0:G * QT, 0:P], negmax[:, g % 2, :], ident[:, :])
                elif what == "O":
                    i = int(name[1])
                    if i == 0:
                        pe.wait_ge(o_norm, 2 * b)
                    for c in range(2):
                        qt = 2 * i + c
                        for k in range(KD):
                            last = nc.tensor.matmul(psM[:, c * D:(c + 1) * D], oN[:, k, qt * P:(qt + 1) * P],
                                                    wo_sb[:, k, :], start=(k == 0), stop=(k == KD - 1))
                elif what == "U":
                    k = int(name[1])
                    if k == 0:
                        pe.wait_ge(ln2, b)
                    for i in range(QT):
                        last = nc.tensor.transpose(psM[:, i * P:(i + 1) * P], h2[:, i, k * P:(k + 1) * P], ident[:, :])
                elif what == "L":
                    for qt in range(QT):
                        for k in range(KD):
                            last = nc.tensor.matmul(psM[:, qt * E:(qt + 1) * E], h2T[:, k, qt * P:(qt + 1) * P],
                                                    wg_sb[:, k, :], start=(k == 0), stop=(k == KD - 1))
                else:
                    pe.wait_ge(choice_done, b)
                    n = 2 * QT * E
                    nc.tensor.matmul(psM[:, 0:n], upper[:, :], choice[:, :, :, :], start=True, stop=True)
                    last = nc.tensor.matmul(psM[:, n:2 * n], ones[:, :], choice[:, :, :, :], start=True, stop=True)
                last.then_inc(job_mm, 1)

            pe.wait_ge(setup, 1)
            pe.wait_ge(wload, 16 * 6)
            pe.wait_ge(ct_in, 16)
            for n, name in enumerate(AHEAD[:-1]):
                job(-1, FIRST, name, n)
            for h in range(LEAD):
                for qt in range(QT):
                    scores_max(0, h, qt)
                if h == G - 1:
                    job(-1, FIRST, "R0n", len(AHEAD) - 1)

            def body(b, kind):
                names = jobs_of(kind)
                for j in range(STEPS):
                    h = j + LEAD
                    ahead = h < NH or kind != LAST
                    hb_ = b + h // NH
                    amid, after = ([n for n in half if n in names] for half in JOBS[j])
                    scores_t(b, j, 0)
                    if ahead:
                        scores_max(hb_, h % NH, 0)
                        scores_max(hb_, h % NH, 1)
                    scores_t(b, j, 1)
                    if j > 0:
                        values(b, j - 1)
                    elif kind != FIRST:
                        values(b - 1, STEPS - 1)
                    for name in amid:
                        job(b, kind, name)
                    scores_t(b, j, 2)
                    if ahead:
                        scores_max(hb_, h % NH, 2)
                        scores_max(hb_, h % NH, 3)
                    scores_t(b, j, 3)
                    for name in after:
                        job(b, kind, name)
            batches(pe, body)
            values(NB - 1, STEPS - 1)
            for name in jobs_of(TAIL):
                job(NB, TAIL, name)

            def expert_of(t):
                return pe.value_load(expert_i[0:1, bass.ds(t, 1)], min_val=0, max_val=E - 1)

            def slot_of(t):
                e = expert_of(t)
                pe.wait_ge(w_ready, e + 1)
                return e % SLOTS

            PARTS = ((0, 0), (1, 0), (0, 1))

            def transpose_tokens(t, u, r):
                pe.wait_ge(g_x[u], 16 * (r + 1))
                wait(pe, x_lo, t)
                for k in range(KD):
                    last = nc.tensor.transpose(psM[:, k * P:(k + 1) * P], X[:, u, k * P:(k + 1) * P], ident[:, :])
                last.then_inc(x_tr, 1)

            def first_product(t, half, slot):
                pe.wait_ge(x_lo, t + 1)
                wait(pe, h_b, 2 * t - 1 + half)
                for k in range(KD):
                    for a, w in PARTS:
                        at_ = k * FF + half * 512
                        last = nc.tensor.matmul(psT[:, half, :], XT[:, a, k, :].bitcast(F32R),
                                                Ws[:, bass.ds(slot, 1), w, at_:at_ + 512].bitcast(F32R),
                                                start=(k == 0 and a + w == 0), stop=(k == KD - 1 and w == 1))
                last.then_inc(h_mm, 1)

            def transpose_hidden(t):
                for half in range(2):
                    pe.wait_ge(h_g, 2 * t + half + 1)
                    wait(pe, h_lo, 2 * t + half - 1)
                    for k in range(4):
                        c = 4 * half + k
                        last = nc.tensor.transpose(psMax[:, 2 + half, k * P:(k + 1) * P], hg[:, c * P:(c + 1) * P],
                                                   ident[:, :])
                    last.then_inc(h_tr, 1)

            def second_product(t, u, slot):
                wait(pe, y_done, t - 1)
                for half in range(2):
                    pe.wait_ge(h_lo, 2 * t + half + 1)
                    for k in range(4):
                        c = 4 * half + k
                        for a, w in PARTS:
                            at_ = HALF + c * D
                            last = nc.tensor.matmul(psMax[:, u % 2, 0:D], hT[:, a, c, :].bitcast(F32R),
                                                    Ws[:, bass.ds(slot, 1), w, at_:at_ + D].bitcast(F32R),
                                                    start=(c == 0 and a + w == 0), stop=(c == KF - 1 and w == 1))
                last.then_inc(y_mm, 1)

            pe.wait_ge(tiles_done, 1)
            pe.sem_inc(y_mm, 1)
            transpose_tokens(0, 0, 0)
            slot = slot_of(0)
            first_product(0, 0, slot)
            first_product(0, 1, slot)
            transpose_tokens(1, 1, 0)
            first_product(1, 0, slot_of(1))
            held = {}

            def expert_step(t, u, r, fresh):
                two = not isinstance(t, int) or t + 2 < TILES
                if fresh:
                    held[0], held[1] = expert_of(t) % SLOTS, expert_of(t + 1) % SLOTS
                transpose_hidden(t)
                if not isinstance(t, int) or t + 1 < TILES:
                    first_product(t + 1, 1, held[1])
                if two:
                    held[2] = slot_of(t + 2)
                    transpose_tokens(t + 2, (u + 2) % RING, r + (u + 2) // RING)
                second_product(t, u, held[0])
                if two:
                    first_product(t + 2, 0, held[2])
                    held[0], held[1] = held[1], held[2]
                else:
                    held[0] = held[1]

            tiles(pe, expert_step)

        @block.scalar
        def _(act):
            def exp_step(b, j, hh):
                n = STEPS * b + j
                if hh == 0:
                    wait(act, pv_mm, n - 1)
                act.wait_ge(st_mm, G * n + hh + 1)
                nc.scalar.activation(probs[:, j % 2, hh, :], psT[:, hh % 2, :], ACT.Exp,
                                     scale=SCALE).then_inc(exp_rd, 1)

            def out_copy(b, g):
                n = NG * b + g
                act.wait_ge(pv_mm, QT * n + QT)
                if not isinstance(b, int) or n >= 2:
                    k = b * 2 + g // 2
                    act.wait_ge(o_out[g % 2], 16 * k)
                nc.scalar.copy(oraw[:, g % 2, :], psO[:, :]).then_inc(o_copy, 1)

            def job(b, kind, name, n=None):
                n = number(b, kind, name) if n is None else n
                what = name[0]
                if what not in "TQKVU":
                    return
                act.wait_ge(job_mm, n + 1)
                i = int(name[1])
                if what == "T":
                    nc.scalar.copy(xnT[:, i, :], psM[:, :]).then_inc(job_rd, 1)
                elif what == "U":
                    nc.scalar.copy(h2T[:, i, :], psM[:, :]).then_inc(job_rd, 1)
                elif what == "V":
                    nc.scalar.copy(V[:, :, i * 8:(i + 1) * 8, 0:DH],
                                   psM[:, :].rearrange("p (t h d) -> p t h d", t=QT, d=DH)).then_inc(job_rd, 1)
                else:
                    wait(act, stored[i], STORES * (b + 1))
                    dst = Qhi if what == "Q" else Khi
                    nc.scalar.copy(dst[:, i, :].bitcast(F32R), psM[:, :]).then_inc(hi_done, 1)

            def split(e, c, half):
                if half == 0:
                    wait(act, w_st[c % 2], 32 * (2 * e + c // 2))
                    act.wait_ge(w_raw[c % 2], 16 * (2 * e + c // 2 + 1))
                cols = slice(half * CHUNK // 2, (half + 1) * CHUNK // 2)
                nc.scalar.copy(whi[:, c % 2, cols].bitcast(F32R), raw[:, c % 2, cols]).then_inc(w_hi, 1)

            act.wait_ge(vset, 2)
            for n, name in enumerate(AHEAD[:-1]):
                job(-1, FIRST, name, n)

            def body(b, kind):
                names = jobs_of(kind)
                for j in range(STEPS):
                    amid, after = ([n for n in half if n in names] for half in JOBS[j])
                    for hh in range(G):
                        exp_step(b, j, hh)
                        if hh == 1 and j % QT == 0:
                            if j > 0:
                                out_copy(b, j // QT - 1)
                            elif kind != FIRST:
                                out_copy(b - 1, NG - 1)
                        if hh == 1:
                            for name in amid:
                                job(b, kind, name)
                        if (j, hh) in SPLITS:
                            split(b, *divmod(SPLITS.index((j, hh)), 2))
                        if (j, hh) == (13, 0) and kind != FIRST:
                            gate(b)
                    for name in after:
                        job(b, kind, name)

            def gate(n):
                act.wait_ge(shifted, n)
                nc.scalar.activation(small[:, 2, :], small[:, 1, :], ACT.Exp).then_inc(gate_exp, 1)

            batches(act, body)
            out_copy(NB - 1, NG - 1)
            for name in jobs_of(TAIL):
                job(NB, TAIL, name)
                if name == "Lp":
                    gate(NB)

            def tokens_copy(t):
                act.wait_ge(x_tr, t + 1)
                wait(act, h_mm, 2 * t)
                nc.scalar.copy(XT[:, 0, :, :].bitcast(F32R), psM[:, 0:D].rearrange("p (k n) -> p k n", k=KD)).then_inc(x_hi, 1)

            def expert_step(t, u, r, fresh):
                for half in range(2):
                    act.wait_ge(h_b, 2 * t + half + 1)
                    wait(act, h_tr, 2 * t - 1 + half)
                    nc.scalar.activation(hg[:, half * 512:(half + 1) * 512], hb[:, half * 512:(half + 1) * 512],
                                         ACT.Gelu).then_inc(h_g, 1)
                for half in range(2):
                    act.wait_ge(h_tr, 2 * t + 1 + half)
                    act.wait_ge(y_mm, t + 1)
                    nc.scalar.copy(hT[:, 0, 4 * half:4 * half + 4, :].bitcast(F32R),
                                   psMax[:, 2 + half, :].rearrange("p (k n) -> p k n", k=4)).then_inc(h_hi, 1)
                if not isinstance(t, int) or t + 2 < TILES:
                    tokens_copy(t + 2)

            for i in range(2):
                act.wait_ge(w_st[i], 32 * 2 * E)
            for e in range(E):
                act.dma_start(b1r[:, e, :], b1[e * FF:(e + 1) * FF].partition_broadcast(P)).then_inc(bload, 16)
            act.dma_start(b2r[:, :, :].rearrange("p e f -> p (e f)"), b2.partition_broadcast(P)).then_inc(bload, 16)
            tokens_copy(0)
            tokens_copy(1)
            tiles(act, expert_step)

        @block.vector
        def _(dve):
            v = nc.vector

            def statistics(src, st, mv, i):
                v.bn_stats(st[:, i, :], src[:, i, :])
                dve.drain()
                return v.bn_aggr(mv[:, i, :], st[:, i, :])

            def finish_statistics(mv, done):
                dve.drain()
                v.tensor_scalar(mv[:, :, 1:2], mv[:, :, 1:2], EPS, None, ALU.add).then_inc(done, 1)

            def take_max(b, h, qt):
                g, hh = h // G, h % G
                dve.wait_ge(smax_mm, 4 * (NH * b + h) + qt + 1)
                v.tensor_reduce(negmax[:, g % 2, hh * QT + qt:hh * QT + qt + 1], psMax[:, qt, :], AX, ALU.max,
                                negate=True).then_inc(max_rd, 1)

            def job(b, kind, name, n=None):
                n = number(b, kind, name) if n is None else n
                what = name[0]
                if what in "TUV":
                    return
                dve.wait_ge(job_mm, n + 1)
                i = int(name[1]) if what not in "LP" else 0
                if what in "QK":
                    before = 0 if isinstance(b, int) and b < 0 else 4 * (b + 1)
                    mine = {"Q0": 1, "K0": 2, "K1": 3, "Q1": 4}[name[:2]]
                    dve.wait_ge(hi_done, before + mine)
                    hi, lo = (Qhi, Qlo) if what == "Q" else (Khi, Klo)
                    v.tensor_tensor(lo[:, i, :].bitcast(F32R), psM[:, :], hi[:, i, :], ALU.subtract).then_inc(job_rd, 1)
                elif what == "R":
                    nb = b + 1 if name[-1] == "n" else b
                    wait(dve, mrow[(i + 2) % NG], 32 * (nb + i // 2))
                    v.tensor_copy(mhi[:, i % 2, :].bitcast(F32R), psM[0:G * QT, 0:P])
                    dve.drain()
                    v.tensor_tensor(mlo[:, i % 2, :].bitcast(F32R), psM[0:G * QT, 0:P], mhi[:, i % 2, :],
                                    ALU.subtract).then_inc(job_rd, 1)
                elif what == "O":
                    if i == 0:
                        dve.wait_ge(xr_in, 16 * b)
                        wait(dve, x1_st, 32 * (b - 1))
                    v.tensor_tensor(x1[:, 2 * i:2 * i + 2, :], psM[:, :].rearrange("p (t d) -> p t d", t=2),
                                    xR[:, 2 * i:2 * i + 2, :], ALU.add).then_inc(x1_done, 1)
                    dve.wait_ge(x1_done, 2 * (b - 1) + i + 1)
                    statistics(x1, bst, mv2, 2 * i).then_inc(job_rd, 1)
                    statistics(x1, bst, mv2, 2 * i + 1)
                    if i == 1:
                        finish_statistics(mv2, ln2_stat)
                elif what == "L":
                    v.tensor_copy(small[:, 0, :], psM[:, 0:QT * E]).then_inc(job_rd, 1)
                else:
                    wait(dve, route, b - 1)
                    v.tensor_copy(prefix[:, :, :, :, :], psM[:, 0:4 * QT * E].rearrange(
                        "p (a k t e) -> p a k t e", a=2, k=2, t=QT)).then_inc(job_rd, 1)

            def sm(i):
                return small[:, i, :].rearrange("p (t e) -> p t e", e=E)

            def wide(i):
                return col[:, i, :].unsqueeze(2).to_broadcast([P, QT, E])

            def second_norm(n, i):
                if i == 0:
                    dve.wait_ge(ln2_rs, n)
                last = v.tensor_scalar(h2[:, i, :], x1[:, i, :], mv2[:, i, 0:1], r2[:, i:i + 1],
                                       ALU.subtract, ALU.mult)
                if i == QT - 1:
                    last.then_inc(ln2, 1)

            def best_of(best, src, t0):
                v.tensor_tensor(sm(t0), src, wide(best), ALU.is_equal)
                dve.drain()
                v.tensor_tensor(sm(t0), sm(t0), rev[:, :, :], ALU.mult)

            def one_hot(dst, t0):
                v.tensor_reduce(col[:, 11, :], sm(t0), AX, ALU.max)
                dve.drain()
                v.tensor_tensor(dst, sm(t0), wide(11), ALU.is_equal)

            def gates(n, part):
                dve.drain()
                if part == 0:
                    v.tensor_reduce(col[:, 0, :], sm(0), AX, ALU.max)
                    dve.drain()
                    v.tensor_tensor(sm(1), sm(0), wide(0), ALU.subtract).then_inc(shifted, 1)
                elif part == 1:
                    dve.wait_ge(gate_exp, n)
                    v.tensor_reduce(col[:, 1, :], sm(2), AX, ALU.add)
                    dve.drain()
                    v.reciprocal(col[:, 2, :], col[:, 1, :])
                    dve.drain()
                    v.tensor_tensor(sm(3), sm(2), wide(2), ALU.mult)
                elif part == 2:
                    v.tensor_reduce(col[:, 3, :], sm(3), AX, ALU.max)
                    dve.drain()
                    best_of(3, sm(3), 4)
                elif part == 3:
                    wait(dve, route, n - 1)
                    one_hot(choice[:, 0, :, :], 4)
                    dve.drain()
                    v.scalar_tensor_tensor(out=sm(5), in0=choice[:, 0, :, :], scalar=-BIG, in1=sm(0),
                                           op0=ALU.mult, op1=ALU.add)
                elif part == 4:
                    v.tensor_reduce(col[:, 4, :], sm(5), AX, ALU.max)
                    dve.drain()
                    best_of(4, sm(5), 6)
                elif part == 5:
                    one_hot(choice[:, 1, :, :], 6)
                    dve.drain()
                    v.tensor_tensor(sm(7), sm(3), choice[:, 1, :, :], ALU.mult).then_inc(choice_done, 1)
                elif part == 6:
                    v.tensor_reduce(col[:, 5, :], sm(7), AX, ALU.add)
                    dve.drain()
                    v.scalar_tensor_tensor(out=col[:, 6, :], in0=col[:, 3, :], scalar=1e-9, in1=col[:, 5, :],
                                           op0=ALU.add, op1=ALU.add)
                    dve.drain()
                    v.reciprocal(col[:, 7, :], col[:, 6, :])
                else:
                    wait(dve, scat, 16 * 2 * QT * (n - 1))
                    v.tensor_tensor(meta[:, :, 0], col[:, 3, :], col[:, 7, :], ALU.mult)
                    v.tensor_tensor(meta[:, :, 1], col[:, 5, :], col[:, 7, :], ALU.mult)
                    v.tensor_copy(meta[:, :, 2].bitcast(I32), idf[:, :])
                    dve.drain()
                    v.tensor_scalar(idf[:, :], idf[:, :], float(T), None, ALU.add)

            def norm_denominators(n):
                dve.wait_ge(den_in, 16 * n)
                v.reciprocal(rden[:, :], den[:, :]).then_inc(den_rd, 1)

            def first_norm(n, i):
                if i == 0:
                    dve.wait_ge(xa_in, 16 * n)
                    wait(dve, ln1, n - 1)
                statistics(xA, ast, mv1, i)
                if i == 3:
                    finish_statistics(mv1, ln1_stat)

            for i in range(QT):
                first_norm(1, i)
            v.memset(Ks[64:98, :, :, :], 1.0)
            v.memset(meta[:, :, :], 0.0)
            dve.wait_ge(wload, 16 * 6)
            v.tensor_scalar(mask_f[:, :], mask_u8[:, :], -1.0, LEFT_OUT, ALU.add, ALU.mult).then_inc(vset, 1)
            v.memset(V[:, :, :, :], 1.0).then_inc(vset, 1)
            v.memset(Qs[64:96, :, :, :], 0.0).then_inc(vset, 1)
            for n, name in enumerate(AHEAD[:-1]):
                job(-1, FIRST, name, n)
            for i in range(QT):
                first_norm(2, i)
            for h in range(LEAD):
                for qt in range(QT):
                    take_max(0, h, qt)
                if h == G - 1:
                    job(-1, FIRST, "R0n", len(AHEAD) - 1)
            dve.wait_ge(empty_st, 48)

            def body(b, kind):
                names = jobs_of(kind)
                for j in range(STEPS):
                    h = j + LEAD
                    ahead = h < NH or kind != LAST
                    amid, after = ([n for n in half if n in names] for half in JOBS[j])
                    for qt in range(QT):
                        if qt == 2:
                            for name in amid:
                                job(b, kind, name)
                        if ahead:
                            take_max(b + h // NH, h % NH, qt)
                        if kind != LAST and (j, qt) in NORM_SLOTS:
                            first_norm(b + 3, NORM_SLOTS.index((j, qt)))
                        if kind != FIRST:
                            if (j, qt) == (2, 2):
                                norm_denominators(b)
                            elif (j, qt) in GATE_SLOTS:
                                gates(b, GATE_SLOTS.index((j, qt)))
                            elif (j, qt) in H2_SLOTS:
                                second_norm(b, H2_SLOTS.index((j, qt)))
                    for name in after:
                        job(b, kind, name)

            batches(dve, body)
            norm_denominators(NB)
            for name in jobs_of(TAIL):
                job(NB, TAIL, name)
                if name == "O1p":
                    for i in range(QT):
                        second_norm(NB, i)
                elif name == "Lp":
                    for part in range(8):
                        gates(NB, part)

            def e_(i):
                return ex[:, i, :].unsqueeze(1).to_broadcast([P, TILES, E])

            dve.wait_ge(pv_mm, 16 * NB)
            dve.wait_ge(route, NB)
            dve.drain()
            v.tensor_tensor(ex[:, 0:2, :], count[:, :, :], base[:, :, :], ALU.subtract)
            dve.drain()
            v.tensor_scalar(ex[:, 2, :], ex[:, 0, :], float(CAP), None, ALU.min)
            dve.drain()
            v.tensor_scalar(ex[:, 3, :], ex[:, 2, :], -1.0, float(CAP), ALU.mult, ALU.add)
            dve.drain()
            v.tensor_tensor(ex[:, 3, :], ex[:, 3, :], ex[:, 1, :], ALU.min)
            dve.drain()
            v.tensor_tensor(ex[:, 4, :], ex[:, 2, :], ex[:, 3, :], ALU.add)
            dve.drain()
            v.tensor_scalar(nint[:, :], ex[:, 4, :], float(P - 1), None, ALU.add)
            dve.drain()
            v.tensor_scalar(nint[:, :], nint[:, :], 7, None, ALU.arith_shift_right)
            dve.drain()
            v.tensor_scalar(ex[:, 5, :], nint[:, :], 1.0, None, ALU.max)
            v.memset(ex[:, 6, :], 1.0)
            dve.drain()
            v.tensor_tensor_scan(ex[:, 7, :], ex[:, 6, :], ex[:, 5, :], 0.0, ALU.mult, ALU.add)
            dve.drain()
            v.tensor_tensor(ex[:, 8, :], ex[:, 7, :], ex[:, 5, :], ALU.subtract)
            dve.drain()
            wide_t = tio[:, :].unsqueeze(2).to_broadcast([P, TILES, E])
            v.tensor_tensor(big[:, 0, :, :], wide_t, e_(8), ALU.is_ge)
            v.tensor_tensor(big[:, 1, :, :], wide_t, e_(7), ALU.is_ge)
            dve.drain()
            v.tensor_reduce(tab[:, 9, :], big[:, 1, :, :], AX, ALU.add)
            v.tensor_tensor(big[:, 0, :, :], big[:, 0, :, :], big[:, 1, :, :], ALU.subtract)
            v.tensor_scalar(after_i[:, :], ex[:, 7, :], 1.0, None, ALU.add)
            dve.drain()
            v.tensor_scalar(expert_i[:, :], tab[:, 9, :], float(E - 1), None, ALU.min)
            dve.drain()
            for i, src in enumerate((e_(8), e_(2), e_(4))):
                v.tensor_tensor(big[:, 1, :, :], big[:, 0, :, :], src, ALU.mult)
                dve.drain()
                v.tensor_reduce(tab[:, i, :], big[:, 1, :, :], AX, ALU.add)
                dve.drain()
            first, kept1, kept, which = (tab[:, i, :] for i in (0, 1, 2, 9))
            v.tensor_tensor(tab[:, 4, :], tio[:, :], first, ALU.subtract)
            dve.drain()
            v.tensor_scalar(tab[:, 4, :], tab[:, 4, :], float(P), pio[:, :], ALU.mult, ALU.add)
            dve.drain()
            v.tensor_tensor(tab[:, 5, :], tab[:, 4, :], kept1, ALU.is_lt)
            v.tensor_tensor(tab[:, 6, :], tab[:, 4, :], kept, ALU.is_lt)
            v.tensor_scalar(tab[:, 7, :], kept1, -1.0, float(REGION), ALU.mult, ALU.add)
            dve.drain()
            v.tensor_scalar(tab[:, 8, :], tab[:, 5, :], -1.0, 1.0, ALU.mult, ALU.add)
            v.tensor_copy(pick[:, :, 0], tab[:, 5, :])
            dve.drain()
            v.tensor_copy(pick[:, :, 1], tab[:, 8, :])
            v.tensor_tensor(tab[:, 7, :], tab[:, 7, :], tab[:, 8, :], ALU.mult)
            dve.drain()
            v.tensor_tensor(tab[:, 4, :], tab[:, 4, :], tab[:, 7, :], ALU.add)
            dve.drain()
            v.scalar_tensor_tensor(out=tab[:, 4, :], in0=which, scalar=float(2 * REGION), in1=tab[:, 4, :],
                                   op0=ALU.mult, op1=ALU.add)
            dve.drain()
            v.tensor_scalar(tab[:, 4, :], tab[:, 4, :], -float(NREG * REGION), None, ALU.add)
            dve.drain()
            v.tensor_tensor(tab[:, 4, :], tab[:, 4, :], tab[:, 6, :], ALU.mult)
            dve.drain()
            v.tensor_scalar(rows_i[:, 0:TILES], tab[:, 4, :], float(NREG * REGION), None, ALU.add)
            v.memset(rows_i[:, TILES:TILES + RING], NREG * REGION)
            dve.drain()
            v.tensor_copy(ex[:, 9, :], ex[:, 0, :]).then_inc(tiles_done, 1)

            def bias(t, half, e):
                dve.wait_ge(h_mm, 2 * t + half + 1)
                wait(dve, h_g, 2 * t - 1 + half)
                v.tensor_tensor(hb[:, half * 512:(half + 1) * 512], psT[:, half, :],
                                b1r[:, bass.ds(e, 1), half * 512:(half + 1) * 512], ALU.add).then_inc(h_b, 1)

            def expert_of(t):
                return dve.value_load(expert_i[0:1, bass.ds(t, 1)], min_val=0, max_val=E - 1)

            def tokens_low(t):
                dve.wait_ge(x_hi, t + 1)
                v.tensor_tensor(XT[:, 1, :, :].bitcast(F32R), psM[:, 0:D].rearrange("p (k n) -> p k n", k=KD),
                                XT[:, 0, :, :], ALU.subtract).then_inc(x_lo, 1)

            held = {}

            def expert_step(t, u, r, fresh):
                if fresh:
                    held[0] = expert_of(t)
                    held[1] = expert_of(t + 1)
                for half in range(2):
                    dve.wait_ge(h_hi, 2 * t + half + 1)
                    cols = slice(4 * half, 4 * half + 4)
                    v.tensor_tensor(hT[:, 1, cols, :].bitcast(F32R), psMax[:, 2 + half, :].rearrange(
                        "p (k n) -> p k n", k=4), hT[:, 0, cols, :], ALU.subtract).then_inc(h_lo, 1)
                if not isinstance(t, int) or t + 1 < TILES:
                    bias(t + 1, 1, held[1])
                two = not isinstance(t, int) or t + 2 < TILES
                if two:
                    tokens_low(t + 2)
                dve.wait_ge(g_meta[u], 16 * (r + 1))
                v.tensor_tensor(wpair[:, u % 2, :], meta_in[:, u, 0:2], pick[:, bass.ds(t, 1), :], ALU.mult)
                dve.drain()
                v.tensor_reduce(wcol[:, u % 2:u % 2 + 1], wpair[:, u % 2, :], AX, ALU.add)
                e = held[0]
                dve.wait_ge(y_mm, t + 2)
                v.tensor_tensor(y0[:, :], psMax[:, u % 2, 0:D], b2r[:, bass.ds(e, 1), :], ALU.add)
                dve.drain()
                wait(dve, added, 16 * (t - 1))
                v.tensor_scalar(y[:, u % 2, :], y0[:, :], wcol[:, u % 2:u % 2 + 1], None, ALU.mult).then_inc(y_done, 1)
                if two:
                    held[2] = expert_of(t + 2)
                    bias(t + 2, 0, held[2])
                    held[0], held[1] = held[1], held[2]
                else:
                    held[0] = held[1]

            dve.wait_ge(tiles_done, 1)
            dve.wait_ge(bload, 16 * (E + 1))
            tokens_low(0)
            e0 = expert_of(0)
            bias(0, 0, e0)
            bias(0, 1, e0)
            tokens_low(1)
            bias(1, 0, expert_of(1))
            tiles(dve, expert_step)

        @block.gpsimd
        def _(pool):
            g = nc.gpsimd
            g.memset(ident[:, :], 0.0)
            g.memset(ones[:, :], 1.0)
            g.memset(upper[:, :], 1.0)
            g.memset(mhalf[:, :], -0.5).then_inc(tio_done, 1)
            pool.wait_ge(tio_done, 1)
            g.affine_select(out=ident[:, :], in_=ident[:, :], compare_op=ALU.not_equal, fill=1.0, base=0,
                            pattern=[[-1, P]], channel_multiplier=1)
            g.affine_select(out=upper[:, :], in_=upper[:, :], compare_op=ALU.is_gt, fill=0.0, base=0,
                            pattern=[[1, P]], channel_multiplier=-1).then_inc(setup, 1)

            def inverse_root(mv, rs, stat, done, n):
                pool.wait_ge(stat, n)
                g.tensor_tensor(rs[:, :], mv[:, :, 1], mhalf[:, :], ALU.pow).then_inc(done, 1)

            def first_norm(n):
                inverse_root(mv1, r1, ln1_stat, ln1_rs, n)
                pool.wait_ge(ln1_rs, n)
                pool.sem_inc(pool_step, 1)
                for i in range(QT):
                    last = g.tensor_scalar(xA[:, i, :], xA[:, i, :], mv1[:, i, 0:1], r1[:, i:i + 1],
                                           ALU.subtract, ALU.mult)
                last.then_inc(ln1, 1)

            def norm_outputs(n):
                pool.wait_ge(rb_in, 32 * n)
                pool.wait_ge(ot_in, 32 * n)
                for half in range(2):
                    g.tensor_tensor(oN[:, half, :], oT[:, half, :], rb[:, half, :], ALU.mult).then_inc(o_norm, 1)

            def split(e, c):
                pool.wait_ge(w_hi, 2 * (4 * e + c + 1))
                g.tensor_tensor(wlo[:, c % 2, :].bitcast(F32R), raw[:, c % 2, :], whi[:, c % 2, :],
                                ALU.subtract).then_inc(w_lo, 1)

            def keep(n):
                pool.wait_ge(ln2, n)
                pool.dma_start(out[n - 1].rearrange("(t p) d -> p t d", p=P), x1[:, :, :]).then_inc(x1_st, 16)
                pool.dma_start(h2d[0:NTOK].rearrange("(b t p) d -> b p t d", b=NB, p=P)[n - 1], h2[:, :, :]).then_inc(x1_st, 16)

            def routes(n, kind):
                pool.wait_ge(job_rd, number(n, kind, "Pp") + 1)
                wait(pool, scat, 16 * 2 * QT * (n - 1))
                pool.sem_inc(pool_step, 1)
                g.tensor_copy(basis[:, :, 0, :], count[:, :, :])
                for t in range(1, QT):
                    pool.drain()
                    g.tensor_tensor(basis[:, :, t, :], basis[:, :, t - 1, :], prefix[:, 1, :, t - 1, :], ALU.add)
                pool.drain()
                g.tensor_tensor(count[:, :, :], basis[:, :, QT - 1, :], prefix[:, 1, :, QT - 1, :], ALU.add)
                g.tensor_tensor(prefix[:, 0, :, :, :], prefix[:, 0, :, :, :], basis[:, :, :, :], ALU.add)
                pool.drain()
                g.tensor_tensor(prefix[:, 0, :, :, :], prefix[:, 0, :, :, :], choice[:, :, :, :], ALU.mult)
                pool.drain()
                for w in (E // 2, E // 4, E // 8):
                    g.tensor_tensor(prefix[:, 0, :, :, 0:w], prefix[:, 0, :, :, 0:w], prefix[:, 0, :, :, w:2 * w],
                                    ALU.add)
                    pool.drain()
                g.tensor_copy(ridx[:, :, :], prefix[:, 0, :, :, 0]).then_inc(route, 1)

            def scatter(n):
                pool.wait_ge(route, n)
                pool.sem_inc(pool_step, 1)
                for k in range(2):
                    for t in range(QT):
                        g.indirect_dma_start(table[:, :], bass.IndirectOffsetOnAxis(
                            ap=ridx[:, k, t:t + 1].bitcast(U32), axis=0), meta[:, t, :], None).then_inc(scat, 16)

            first_norm(1)
            g.memset(fill0[:, :, :], 0.0)
            g.memset(rb[:, :, :], 0.0).then_inc(tio_done, 1)
            pool.wait_ge(tio_done, 2)
            g.memset(fill0[:, :, 2:3].bitcast(I32), NTOK).then_inc(tio_done, 1)
            pool.wait_ge(tio_done, 3)
            pool.dma_start(table[0:NREG * REGION].rearrange("(p r) c -> p r c", p=P), fill0[:, :, :]).then_inc(empty_st, 16)
            pool.dma_start(table[NREG * REGION:], fill0[:, 0, :]).then_inc(empty_st, 16)
            pool.dma_start(h2d[NTOK:], rb[:, 0, 0:D]).then_inc(empty_st, 16)
            g.iota(rev[:, :, :], [[0, QT], [-1, E]], base=E, channel_multiplier=0, allow_small_or_imprecise_dtypes=True)
            g.iota(idf[:, :], [[P, QT]], base=0, channel_multiplier=1, allow_small_or_imprecise_dtypes=True)
            g.iota(base[:, :, :], [[REGION, 2], [2 * REGION, E]], base=0, channel_multiplier=0,
                   allow_small_or_imprecise_dtypes=True)
            g.iota(count[:, :, :], [[REGION, 2], [2 * REGION, E]], base=0, channel_multiplier=0,
                   allow_small_or_imprecise_dtypes=True)
            g.iota(tio[:, :], [[1, TILES]], base=0, channel_multiplier=0, allow_small_or_imprecise_dtypes=True)
            g.iota(pio[:, :], [[0, 1]], base=0, channel_multiplier=1,
                   allow_small_or_imprecise_dtypes=True).then_inc(tio_done, 1)
            first_norm(2)
            pool.wait_ge(empty_st, 48)

            def body(b, kind):
                split(b, 0)
                if kind != FIRST:
                    norm_outputs(b)
                if kind != LAST:
                    first_norm(b + 3)
                split(b, 1)
                if kind != FIRST:
                    inverse_root(mv2, r2, ln2_stat, ln2_rs, b)
                    keep(b)
                split(b, 2)
                split(b, 3)
                if kind != FIRST:
                    routes(b, kind)
                    scatter(b)

            batches(pool, body)
            norm_outputs(NB)
            inverse_root(mv2, r2, ln2_stat, ln2_rs, NB)
            keep(NB)
            routes(NB, TAIL)
            scatter(NB)

            def gather_meta(t, u):
                g.tensor_copy(rowidx[:, u:u + 1], rows_i[:, bass.ds(t, 1)]).then_inc(rix, 1)
                pool.wait_ge(rix, t + 1)
                pool.sem_inc(pool_step, 1)
                g.indirect_dma_start(meta_in[:, u, :], None, table[:, :], bass.IndirectOffsetOnAxis(
                    ap=rowidx[:, u:u + 1].bitcast(U32), axis=0)).then_inc(g_meta[u], 16)

            def gather_tokens(t, u, r):
                pool.wait_ge(g_meta[u], 16 * (r + 1))
                wait(pool, x_tr, t - RING + 1)
                pool.sem_inc(pool_step, 1)
                g.indirect_dma_start(X[:, u, :], None, h2d[:, :], bass.IndirectOffsetOnAxis(
                    ap=meta_in[:, u, 2:3].bitcast(U32), axis=0)).then_inc(g_x[u], 16)

            pool.wait_ge(tiles_done, 1)
            pool.wait_ge(scat, 16 * 2 * QT * NB)
            pool.wait_ge(x1_st, 32 * NB)
            for t in range(RING - 1):
                gather_meta(t, t)
            for t in range(3):
                gather_tokens(t, t, 0)
            out_rows = out.rearrange("b t d -> (b t) d")

            def expert_step(t, u, r, fresh):
                if not isinstance(t, int) or t + 3 < TILES:
                    gather_tokens(t + 3, (u + 3) % RING, r + (u + 3) // RING)
                wait(pool, added, 16 * t)
                if not isinstance(t, int) or t + RING - 1 < TILES:
                    gather_meta(t + RING - 1, (u + RING - 1) % RING)
                pool.wait_ge(y_done, t + 1)
                pool.sem_inc(pool_step, 1)
                g.indirect_dma_start(out_rows, bass.IndirectOffsetOnAxis(ap=meta_in[:, u, 2:3].bitcast(U32), axis=0),
                                     y[:, u % 2, :], None, compute_op=ALU.add, bounds_check=NTOK - 1,
                                     oob_is_err=False).then_inc(added, 16)

            tiles(pool, expert_step)
            pool.wait_ge(added, 16 * TILES)


def kernel(x, ctx_1024, mask_Bx1x1xS2_bf1, L0_xattn_Wq, L0_xattn_Wk, L0_xattn_Wv, L0_xattn_Wo,
           L0_ffn_Wg, L0_ffn_W1, L0_ffn_b1, L0_ffn_W2, L0_ffn_b2):
    import numpy as np
    import concourse.bacc as bacc
    from concourse.bass_utils import run_bass_kernel_spmd

    arrays = {
        "x": np.asarray(x),
        "ctxT": np.ascontiguousarray(np.asarray(ctx_1024).transpose(0, 2, 1)),
        "mask": np.asarray(mask_Bx1x1xS2_bf1).reshape(NB, T).view(np.uint8),
        "WqT": np.ascontiguousarray(np.asarray(L0_xattn_Wq).T),
        "WkT": np.ascontiguousarray(np.asarray(L0_xattn_Wk).T),
        "WvT": np.ascontiguousarray(np.asarray(L0_xattn_Wv).T),
        "WoT": np.ascontiguousarray(np.asarray(L0_xattn_Wo).T),
        "Wg": np.asarray(L0_ffn_Wg), "W1": np.asarray(L0_ffn_W1),
        "b1": np.asarray(L0_ffn_b1).reshape(-1), "W2": np.asarray(L0_ffn_W2),
        "b2": np.asarray(L0_ffn_b2).reshape(-1),
    }
    nc = bacc.Bacc("TRN2", target_bir_lowering=False, num_devices=1)
    args = [nc.dram_tensor(n, a.shape, mybir.dt.from_np(a.dtype), kind="ExternalInput").ap()
            for n, a in arrays.items()]
    out = nc.dram_tensor("out", (NB, T, D), F32, kind="ExternalOutput").ap()
    build(nc, *args, out)
    r = run_bass_kernel_spmd(nc, [arrays], core_ids=[0])
    return r.results[0]["out"]
```
